# Optimizing a Trainium2 kernel written in Bass

```python
import numpy as np
import jax
import jax.numpy as jnp

def _softmax(x, axis=-1):
    return jax.nn.softmax(x, axis=axis)

def _gelu(x):
    return jax.nn.gelu(x, approximate=True)

def _silu(x):
    return jax.nn.silu(x)

def _sigmoid(x):
    return jax.nn.sigmoid(x)

def _layernorm(x, axis=-1, eps=1e-05):
    m = jnp.mean(x, axis=axis, keepdims=True)
    v = jnp.var(x, axis=axis, keepdims=True)
    return (x - m) / jnp.sqrt(v + eps)

def _scatter_add(tgt, idx, src, axis=0):
    return tgt.at[idx].add(src)

def _segment_sum(src, seg, n):
    return jax.ops.segment_sum(src, seg, n)
kernel_name = 'mk_xattn_ffn_d1_seqx_r4_0881f4'

def setup_inputs(seed: int=0):
    np.random.seed(seed)
    _w = jnp.asarray

    def _rec_inputs():
        import jax
        import jax.numpy as jnp
        _rk = jax.random.key(seed)
        x = 0.5 + 0.2887 * jax.random.normal(jax.random.fold_in(_rk, 1), (4, 512, 512), jnp.float32)
        _lenS = 512 - jax.random.randint(jax.random.fold_in(_rk, 7), (4,), 0, max(1, 512 // 4) + 1, jnp.int32)
        _lenS2 = 512 - jax.random.randint(jax.random.fold_in(_rk, 8), (4,), 0, max(1, 512 // 4) + 1, jnp.int32)
        _ctx_512P = jax.random.normal(jax.random.fold_in(_rk, 11), (4, 16, 128), jnp.float32)
        _ctx_512c = jax.random.dirichlet(jax.random.fold_in(_rk, 511), 0.3 * jnp.ones((16,), jnp.float32), (4, 512))
        _ctx_512t = jnp.einsum('bsk,bkd->bsd', _ctx_512c, _ctx_512P)
        _ctx_512t = _ctx_512t * jax.lax.rsqrt(jnp.mean(jnp.square(_ctx_512t)) + 1e-12) * 0.953939
        ctx_512 = -0.000392918 + 0.999932 * (_ctx_512t + 0.3 * jax.random.normal(jax.random.fold_in(_rk, 611), (4, 512, 128), jnp.float32))
        return (x, ctx_512)
    x, ctx_512 = _rec_inputs()

    def _L0_xattn_setup():
        import jax, jax.numpy as jnp
        import numpy as np
        B, N, D = (16, 512, 128)
        H = 4
        TOP_K_RATIO = 0.3
        key = jax.random.key(seed)
        k1, k2, k3, k4 = jax.random.split(key, 4)
        h = jax.random.normal(k1, (B, N, D), dtype=jnp.float32)
        adj_raw = jax.random.uniform(k2, (B, N, N), dtype=jnp.float32)
        lim = 1.0 / np.sqrt(D)
        Wq = jax.random.uniform(k3, (D, D), minval=-lim, maxval=lim, dtype=jnp.float32)
        Wk = jax.random.uniform(k4, (D, D), minval=-lim, maxval=lim, dtype=jnp.float32)
        gamma_raw = jnp.float32(-0.85)
        return {'h': h, 'adj_raw': adj_raw, 'Wq': Wq, 'Wk': Wk, 'gamma_raw': gamma_raw}
    _L0_xattn_all = _L0_xattn_setup()
    _L0_xattn_in = {k: v for k, v in _L0_xattn_all.items() if k in ('Wq', 'Wk', 'gamma_raw')}
    del _L0_xattn_all

    def _L0_ffn_setup():
        import jax, jax.numpy as jnp
        import numpy as np
        ALPHA = 1.702
        LIMIT = 7.0
        TOP_K = 4
        B, S, H = (1, 256, 512)
        E, D = (16, 512)
        key = jax.random.key(seed)
        ks = jax.random.split(key, 7)
        s = 0.02
        return {'hidden_states': jax.random.normal(ks[0], (B, S, H), dtype=jnp.float32), 'router_weight': jax.random.normal(ks[1], (E, H), dtype=jnp.float32) * s, 'router_bias': jax.random.normal(ks[2], (E,), dtype=jnp.float32) * s, 'gate_up_proj': jax.random.normal(ks[3], (E, H, 2 * D), dtype=jnp.float32) * s, 'gate_up_proj_bias': jax.random.normal(ks[4], (E, 2 * D), dtype=jnp.float32) * s, 'down_proj': jax.random.normal(ks[5], (E, D, H), dtype=jnp.float32) * s, 'down_proj_bias': jax.random.normal(ks[6], (E, H), dtype=jnp.float32) * s}
    _L0_ffn_all = _L0_ffn_setup()
    _L0_ffn_in = {k: v for k, v in _L0_ffn_all.items() if k in ('router_weight', 'router_bias', 'gate_up_proj', 'gate_up_proj_bias', 'down_proj', 'down_proj_bias')}
    del _L0_ffn_all
    return {'x': x, 'ctx_512': ctx_512, 'L0_xattn_Wq': _L0_xattn_in['Wq'], 'L0_xattn_Wk': _L0_xattn_in['Wk'], 'L0_xattn_gamma_raw': _L0_xattn_in['gamma_raw'], 'L0_ffn_router_weight': _L0_ffn_in['router_weight'], 'L0_ffn_router_bias': _L0_ffn_in['router_bias'], 'L0_ffn_gate_up_proj': _L0_ffn_in['gate_up_proj'], 'L0_ffn_gate_up_proj_bias': _L0_ffn_in['gate_up_proj_bias'], 'L0_ffn_down_proj': _L0_ffn_in['down_proj'], 'L0_ffn_down_proj_bias': _L0_ffn_in['down_proj_bias']}

def reference(x, ctx_512, L0_xattn_Wq, L0_xattn_Wk, L0_xattn_gamma_raw, L0_ffn_router_weight, L0_ffn_router_bias, L0_ffn_gate_up_proj, L0_ffn_gate_up_proj_bias, L0_ffn_down_proj, L0_ffn_down_proj_bias):
    import jax
    import jax.numpy as jnp

    def _L0_xattn_ref(h, adj_raw, Wq, Wk, gamma_raw):
        import jax, jax.numpy as jnp
        import numpy as np
        B, N, D = (16, 512, 128)
        H = 4
        TOP_K_RATIO = 0.3
        b, n, dm = h.shape
        d = dm // H
        Q = (h @ Wq.T).reshape(b, n, H, d).transpose(0, 2, 1, 3)
        K = (h @ Wk.T).reshape(b, n, H, d).transpose(0, 2, 1, 3)
        sim = jnp.einsum('bhnd,bhmd->bnm', Q, K) / (jnp.sqrt(jnp.float32(d)) * H)
        k = max(1, int(n * TOP_K_RATIO))
        topk_vals = jax.lax.top_k(sim, k)[0]
        threshold = topk_vals[:, :, -1:]
        sparse_mask = (sim >= threshold).astype(sim.dtype)
        A_learned = jax.nn.sigmoid(sim) * sparse_mask
        A_learned = (A_learned + jnp.swapaxes(A_learned, -1, -2)) * 0.5
        gamma = jax.nn.sigmoid(gamma_raw)
        return (1.0 - gamma) * adj_raw + gamma * A_learned

    def _L0_ffn_ref(hidden_states, router_weight, router_bias, gate_up_proj, gate_up_proj_bias, down_proj, down_proj_bias):
        import jax, jax.numpy as jnp
        import numpy as np
        ALPHA = 1.702
        LIMIT = 7.0
        TOP_K = 4
        B, S, H = (1, 256, 512)
        E, D = (16, 512)
        batch, seq, hdim = hidden_states.shape
        x = hidden_states.reshape(-1, hdim)
        T = x.shape[0]
        logits = x @ router_weight.T + router_bias
        top_val, top_idx = jax.lax.top_k(logits, TOP_K)
        top_val = jax.nn.softmax(top_val, axis=-1)
        router_scores = jnp.zeros_like(logits).at[jnp.arange(T)[:, None], top_idx].set(top_val)
        gate_up = jnp.einsum('th,ehd->etd', x, gate_up_proj) + gate_up_proj_bias[:, None, :]
        gate = gate_up[..., ::2]
        up = gate_up[..., 1::2]
        gate = jnp.minimum(gate, LIMIT)
        up = jnp.clip(up, -LIMIT, LIMIT)
        glu = gate * jax.nn.sigmoid(gate * ALPHA)
        out = jnp.einsum('etd,edh->eth', (up + 1.0) * glu, down_proj) + down_proj_bias[:, None, :]
        out = out * router_scores.T[:, :, None]
        out = out.sum(axis=0)
        return out.reshape(batch, seq, hdim)
    x = x + _L0_xattn_ref(ctx_512, _layernorm(x, axis=-1), L0_xattn_Wq, L0_xattn_Wk, L0_xattn_gamma_raw)
    x = x + _L0_ffn_ref(_layernorm(x, axis=-1), L0_ffn_router_weight, L0_ffn_router_bias, L0_ffn_gate_up_proj, L0_ffn_gate_up_proj_bias, L0_ffn_down_proj, L0_ffn_down_proj_bias)
    return x

_drawn_inputs = setup_inputs


def setup_inputs(seed=0):
    import zlib

    import numpy as np

    out = dict(_drawn_inputs(seed))
    spreads = {}
    factors = {'L0_ffn_router_bias': 6.067,
     'L0_ffn_gate_up_proj_bias': 8.0,
     'L0_ffn_down_proj_bias': 6.205}
    for name, (base, spread) in spreads.items():
        noise = np.random.default_rng([zlib.crc32(name.encode()), seed]).standard_normal(out[name].shape)
        drawn = base * np.exp(spread * noise) if base else spread * noise
        out[name] = jnp.asarray(drawn.astype(out[name].dtype))
    for name, factor in factors.items():
        out[name] = (out[name] * factor).astype(out[name].dtype)
    return out
```

```python
import concourse.bass as bass
from concourse import mybir
from contextlib import ExitStack

P = 128
NB, N, H = 4, 512, 512
C = 128
HEADS = 4
E, TOP_K, D = 16, 4, 512
RT = N // P
NT = NB * RT
TOKENS = NB * N
HC = H // P
KEEP = max(1, int(N * 0.3))
SIM_SCALE = 1.0 / ((C // HEADS) ** 0.5 * HEADS)
ALPHA, LIMIT = 1.702, 7.0
EPS = 1e-5
NEG = -3.0e38
UNROLL = 4
TILES = -(-(TOKENS * TOP_K // P + E - 1) // UNROLL) * UNROLL
SLOTS = E * TOKENS
GU = 2 * D
TABLE = TILES + 2


def xattn_moe_kernel(nc, x, ctx_in, wq, wk, gamma_raw, rw, rb, gup, gupb, dwn, dwnb, out):
    fp32, u32, i32 = mybir.dt.float32, mybir.dt.uint32, mybir.dt.int32
    ALU = mybir.AluOpType
    ACT = mybir.ActivationFunctionType
    AX = mybir.AxisListType

    x_v = x.rearrange("b (r p) h -> p (b r) h", p=P)
    ctx_v = ctx_in.rearrange("b (r p) c -> p (b r) c", p=P)
    out_v = out.rearrange("b n h -> (b n) h")
    gup_v = gup.rearrange("e (c p) d -> e p c d", p=P)
    dwn_v = dwn.rearrange("e (c p) h -> e p c h", p=P)

    xn_d = nc.dram_tensor("xn_rows", [TOKENS + P, H], fp32, kind="Internal").ap()
    acc_d = nc.dram_tensor("acc_rows", [TOKENS + P, H], fp32, kind="Internal").ap()
    slot_d = nc.dram_tensor("slot_rows", [SLOTS + P, 2], u32, kind="Internal").ap()

    ctx = ExitStack()
    with ctx:
        def sb(name, shape, dt=fp32):
            return ctx.enter_context(nc.sbuf_tensor(name, shape, dt))

        def sem(name):
            return ctx.enter_context(nc.semaphore(name))

        banks = [ctx.enter_context(nc.psum_tensor(f"bank{i}", [P, 512], fp32)) for i in range(2)]
        bank67 = [ctx.enter_context(nc.psum_tensor(f"bank{i}", [P, 512], fp32)) for i in range(2, 4)]
        psG = [ctx.enter_context(nc.psum_tensor(f"gate_up_ps{i}", [P, GU], fp32)) for i in range(2)]
        ps_q, ps_k = banks
        ps_s = bank67
        ps_at = psG[0][:, 0:512]
        ps_xt = psG[0][:, 512:1024]
        ps_bd = psG[1][:, 0:512]
        ps_m = psG[1][:, 512:1024]
        ps_logit = ps_m[:, 0:RT * E]
        ps_rank = ps_m[:, 64:64 + RT * E]
        ps_rw = ps_m[:, 128:128 + HC * E]
        ps_scT = ps_m[0:E, 256:256 + P]
        ps_x, ps_h = banks
        ps_y = bank67

        x_sb = sb("x_sb", [P, NT, H])
        ctx_sb = sb("ctx_sb", [P, NT, C])
        wq_sb, wk_sb = sb("wq_sb", [P, C]), sb("wk_sb", [P, C])
        wqT, wkT = sb("wqT", [P, C]), sb("wkT", [P, C])
        rw_sb = sb("rw_sb", [E, H])
        rwT = sb("rwT", [P, HC * E])
        rb_sb = sb("rb_sb", [P, E])
        bd_sb = sb("bd_sb", [E, H])
        ident = sb("ident", [P, P])
        lower = sb("lower", [P, P])
        ones = sb("ones", [P, P])
        iota_e = sb("iota_e", [P, E])
        slot0_e = sb("slot0_e", [P, E])
        token_id = sb("token_id", [P, NT], i32)
        pad_i = sb("pad_i", [P, (SLOTS + P) // P], i32)
        pad_rows = sb("pad_rows", [P, (SLOTS + P) // P, 2], i32)
        zero_rows = sb("zero_rows", [P, H])
        gam = sb("gam", [P, 4])
        eps_c = sb("eps_c", [P, 1])
        ctxT, qT, kT = sb("ctxT", [P, N]), sb("qT", [P, N]), sb("kT", [P, N])
        sim = sb("sim", [P, 2, RT, N])
        work = sb("work", [P, N])
        top8 = sb("top8", [P, 8])
        thr = sb("thr", [P, RT])
        A = sb("A", [P, RT, N])
        base = sb("base", [P, RT, N])
        x1 = sb("x1", [P, RT, N])
        xn2 = sb("xn2", [P, RT, N])
        xn2T = sb("xn2T", [P, RT, N])
        st = sb("st", [P, RT, 6])
        mv = sb("mv", [P, RT, 2])
        sd = sb("sd", [P, RT])
        rs = sb("rs", [P, RT])
        s1, b1 = sb("s1", [P, RT]), sb("b1", [P, RT])
        r2, b2 = sb("r2", [P, RT]), sb("b2", [P, RT])
        logit = sb("logit", [P, RT, E])
        best = sb("best", [P, RT, 8])
        best_i = sb("best_i", [P, RT, 8], u32)
        ek = sb("ek", [P, RT, TOP_K])
        dl = sb("dl", [P, RT, TOP_K])
        ex = sb("ex", [P, RT, TOP_K])
        den = sb("den", [P, RT])
        score = sb("score", [P, RT, TOP_K])
        hot = sb("hot", [P, RT, TOP_K, E])
        hotv = sb("hotv", [P, RT, TOP_K, E])
        onehot = sb("onehot", [P, RT, E])
        before = sb("before", [P, NT + 1, E])
        dense = sb("dense", [P, RT, E])
        denseT = sb("denseT", [E, P])
        pos = sb("pos", [P, RT, E])
        posk = sb("posk", [P, RT, TOP_K])
        slot_i = sb("slot_i", [P, NT * TOP_K], u32)
        payload = sb("payload", [P, NT * TOP_K, 2], u32)
        base_out = sb("base_out", [P, RT, N])
        cnt = sb("cnt", [1, E])
        ncmp = sb("ncmp", [1, E, E])
        jtab = sb("jtab", [1, E])
        til = sb("til", [1, E])
        cum = sb("cum", [1, 2, E])
        ttab = sb("ttab", [1, TABLE])
        alt = sb("alt", [1, E])
        cmp_t = sb("cmp_t", [1, TABLE, E])
        cmp_w = sb("cmp_w", [1, TABLE, E])
        tf = sb("tf", [1, 6, TABLE])
        tile_tab = sb("tile_tab", [1, 4, TABLE], i32)
        end_tab = sb("end_tab", [1, E], i32)
        wgu = sb("wgu", [P, 2, HC, GU])
        wdn = sb("wdn", [P, 2, HC, H])
        bgu = sb("bgu", [P, 2, GU])
        slot_sb = sb("slot_sb", [P, UNROLL, 2], u32)
        xg = x_sb[:, 0:2, :]
        xT = x_sb[:, 2:4, :]
        gu = x_sb[:, 4:6, :].rearrange("p a h -> p (a h)")
        gc = x_sb[:, 6, :]
        uc = x_sb[:, 7, :]
        sg = x_sb[:, 8, :]
        h1 = x_sb[:, 9, :]
        hb = x_sb[:, 10:12, :]
        hT = x_sb[:, 12:14, :]
        yb = x_sb[:, 14:16, :]

        S = {}
        for name in ("const_in", "ctx_in_s", "bias_in", "pad_out", "pool_c", "dve_c", "wT_ps", "wT_done", "gam_done",
                     "ctxT_ps", "ctxT_done", "q_ps", "k_ps", "qk_done", "s_ps", "s_done", "sig_done",
                     "a_done", "at_ps", "x1_done", "var1", "sd1", "aff1", "base_done", "var2", "sd2", "aff2",
                     "xn2_done", "xn2_out", "xt_ps", "xt_done", "logit_ps", "dl_done", "ex_done", "hot_done",
                     "rank_ps", "dense_done", "scT_ps", "scT_done", "bd_ps", "bo_done", "acc_out", "slots_done",
                     "payload_done", "scat", "chain", "cnt_ps", "table_done",
                     "w0_in", "w1_in", "gathered0", "gathered1", "xT_ps", "xT_done", "gu_ps", "gu_read", "gc_done", "sg_done",
                     "h_done", "hT_ps", "hT_done", "y_ps", "y_done", "added",
                     "fin", "achain", "pchain"):
            S[name] = sem(name)
        x_in = [sem(f"x_in{b}") for b in range(NB)]
        slots_in = [sem(f"slots_in{k}") for k in range(UNROLL)]
        block = ctx.enter_context(nc.Block())

        @block.sync
        def _(sp):
            sp.dma_start(ctx_sb[:], ctx_v).then_inc(S["ctx_in_s"], 16)
            sp.dma_start(wq_sb[:], wq).then_inc(S["const_in"], 16)
            sp.dma_start(wk_sb[:], wk).then_inc(S["const_in"], 16)
            sp.dma_start(rw_sb[:], rw).then_inc(S["const_in"], 16)
            sp.dma_start(bd_sb[:], dwnb).then_inc(S["const_in"], 16)
            sp.dma_start(rb_sb[:], rb.rearrange("(a e) -> a e", a=1).broadcast_to([P, E])).then_inc(S["const_in"], 16)
            sp.dma_start(gam[:, 0:1], gamma_raw.rearrange("(a e) -> a e", a=1).broadcast_to([P, 1])).then_inc(S["const_in"], 16)
            for b in range(NB):
                sp.dma_start(x_sb[:, b * RT:(b + 1) * RT, :], x_v[:, b * RT:(b + 1) * RT, :]).then_inc(x_in[b], 16)
            sp.wait_ge(S["dve_c"], 3)
            sp.dma_start(slot_d.rearrange("(p a) t -> p a t", p=P), pad_rows[:].bitcast(u32)).then_inc(S["pad_out"], 16)
            sp.dma_start(xn_d[TOKENS:TOKENS + P, :], zero_rows[:]).then_inc(S["pad_out"], 16)
            sp.dma_start(acc_d[TOKENS:TOKENS + P, :], zero_rows[:]).then_inc(S["pad_out"], 16)

            def load_expert(e, par):
                done = S["w1_in"] if par else S["w0_in"]
                sp.dma_start(wgu[:, par], gup_v[e]).then_inc(done, 16)
                sp.dma_start(wdn[:, par], dwn_v[e]).then_inc(done, 16)
                sp.dma_start(bgu[:, par], gupb[e:e + 1, :].broadcast_to([P, GU])).then_inc(done, 16)

            load_expert(0, 0)
            load_expert(1, 1)
            for b in range(NB):
                rows = slice(b * N, (b + 1) * N)
                sp.wait_ge(S["xn2_done"], RT * (b + 1))
                sp.dma_start(xn_d[rows, :].rearrange("(r p) h -> p r h", p=P), xn2[:]).then_inc(S["xn2_out"], 16)
                sp.wait_ge(S["bo_done"], RT * (b + 1))
                sp.dma_start(acc_d[rows, :].rearrange("(r p) h -> p r h", p=P), base_out[:]).then_inc(S["acc_out"], 16)
            sp.wait_ge(S["table_done"], 1)
            with sp.Fori(1, E // 2) as i:
                for par in range(2):
                    end = sp.value_load(end_tab[0:1, bass.ds(2 * i + (par - 2), 1)], min_val=0, max_val=TILES)
                    sp.wait_ge(S["y_ps"], end + 1)
                    e = 2 * i + par
                    done = S["w1_in"] if par else S["w0_in"]
                    sp.dma_start(wgu[:, par], gup_v[bass.ds(e, 1)].rearrange("a p c d -> p (a c) d")).then_inc(done, 16)
                    sp.dma_start(wdn[:, par], dwn_v[bass.ds(e, 1)].rearrange("a p c d -> p (a c) d")).then_inc(done, 16)
                    sp.dma_start(bgu[:, par], gupb[bass.ds(e, 1), :].broadcast_to([P, GU])).then_inc(done, 16)
            sp.wait_ge(S["added"], 16 * TILES)
            sp.dma_start(out_v, acc_d[0:TOKENS, :]).then_inc(S["fin"], 16)
            sp.wait_ge(S["fin"], 16)

        @block.gpsimd
        def _(pool):
            c = S["pool_c"]
            pool.memset(ident[:], 0.0).then_inc(c, 1)
            pool.memset(lower[:], 1.0).then_inc(c, 1)
            pool.memset(ones[:], 1.0).then_inc(c, 1)
            pool.wait_ge(c, 3)
            pool.affine_select(out=ident[:], in_=ident[:], compare_op=ALU.not_equal, fill=1.0, base=0,
                               pattern=[[-1, P]], channel_multiplier=1).then_inc(c, 1)
            pool.affine_select(out=lower[:], in_=lower[:], compare_op=ALU.is_gt, fill=0.0, base=0,
                               pattern=[[1, P]], channel_multiplier=-1).then_inc(c, 1)
            kw = dict(allow_small_or_imprecise_dtypes=True)
            pool.iota(iota_e[:], pattern=[[1, E]], base=0, channel_multiplier=0, **kw).then_inc(c, 1)
            pool.iota(slot0_e[:], pattern=[[TOKENS, E]], base=0, channel_multiplier=0, **kw).then_inc(c, 1)
            pool.iota(token_id[:], pattern=[[P, NT]], base=0, channel_multiplier=1).then_inc(c, 1)
            pool.iota(pad_i[:], pattern=[[1, (SLOTS + P) // P]], base=0, channel_multiplier=1).then_inc(c, 1)
            pool.iota(jtab[:], pattern=[[P, E]], base=0, channel_multiplier=0, **kw).then_inc(c, 1)
            pool.iota(ttab[:], pattern=[[1, TABLE]], base=0, channel_multiplier=0, **kw).then_inc(c, 1)
            pool.memset(alt[:], -1.0).then_inc(c, 1)
            pool.wait_ge(c, 12)
            pool.memset(alt[:, 0:E:2], 1.0).then_inc(c, 1)
            pool.wait_ge(S["pad_out"], 48)
            for b in range(NB):
                pool.wait_ge(S["payload_done"], b + 1)
                for k in range(b * RT * TOP_K, (b + 1) * RT * TOP_K):
                    pool.indirect_dma_start(slot_d, bass.IndirectOffsetOnAxis(slot_i[:, k:k + 1], 0),
                                            payload[:, k, :], None).then_inc(S["scat"], 16)
            pool.wait_ge(S["scat"], 16 * NT * TOP_K)
            pool.sem_inc(S["slots_done"], 1)
            pool.wait_ge(S["xn2_out"], 16 * NB)
            pool.wait_ge(S["acc_out"], 16 * NB)

            def gather(T, k):
                gathered = S[f"gathered{k % 2}"]
                pool.indirect_dma_start(xg[:, k % 2, :], None, xn_d,
                                        bass.IndirectOffsetOnAxis(slot_sb[:, k, 0:1], 0)).then_inc(gathered, 16)

            def add(T, k):
                pool.indirect_dma_start(acc_d, bass.IndirectOffsetOnAxis(slot_sb[:, k, 0:1], 0),
                                        yb[:, k % 2, :], None, compute_op=ALU.add).then_inc(S["added"], 16)

            def step(T, k, first=False, last=False):
                nk, pk = (k + 1) % UNROLL, (k - 1) % UNROLL
                if not last:
                    pool.wait_ge(slots_in[nk], 16 * ((T + 1 - nk) // UNROLL + 1) if isinstance(T, int) else 4 * (T + 1 - nk) + 16)
                    if not first:
                        pool.wait_ge(S["xT_ps"], T)
                    pool.sem_inc(S["pchain"], 1)
                    gather(T + 1, nk)
                if not first:
                    pool.wait_ge(S["y_done"], T)
                    if not (isinstance(T, int) and T == 1):
                        pool.wait_ge(S["added"], 16 * (T - 1))
                    pool.sem_inc(S["pchain"], 1)
                    add(T - 1, pk)

            pool.wait_ge(slots_in[0], 16)
            gather(0, 0)
            for T in range(UNROLL):
                step(T, T, first=(T == 0))
            with pool.Fori(1, TILES // UNROLL) as lap:
                for k in range(UNROLL - 1):
                    step(UNROLL * lap + k, k)
                k = UNROLL - 1
                T = UNROLL * lap + k
                step(T, k)
            pool.wait_ge(S["y_done"], TILES)
            pool.wait_ge(S["added"], 16 * (TILES - 1))
            add(TILES - 1, UNROLL - 1)
            pool.wait_ge(S["gathered0"], 16 * (TILES // 2 + 1))
            pool.wait_ge(slots_in[1], 16 * (TILES // UNROLL + 1))

        @block.scalar
        def _(act):
            n = [0]

            def link(ins):
                n[0] += 1
                ins.then_inc(S["achain"], 1)
                act.wait_ge(S["achain"], n[0])

            act.wait_ge(S["const_in"], 96)
            nc.scalar.activation(gam[:, 1:2], gam[:, 0:1], ACT.Sigmoid).then_inc(S["gam_done"], 1)

            def front(b):
                act.wait_ge(S["ctxT_ps"], b + 1)
                if b:
                    act.wait_ge(S["k_ps"], b)
                nc.scalar.copy(ctxT[:], ps_q[:]).then_inc(S["ctxT_done"], 1)
                if b:
                    act.wait_ge(S["s_ps"], RT * b)
                act.wait_ge(S["q_ps"], b + 1)
                nc.scalar.copy(qT[:], ps_q[:]).then_inc(S["qk_done"], 1)
                act.wait_ge(S["k_ps"], b + 1)
                nc.scalar.copy(kT[:], ps_k[:]).then_inc(S["qk_done"], 1)
                for r in range(RT):
                    i = RT * b + r
                    act.wait_ge(S["s_ps"], i + 1)
                    if b >= 2:
                        act.wait_ge(S["a_done"], RT * (b - 1))
                    nc.scalar.copy(sim[:, b % 2, r, :], ps_s[i % 2][:]).then_inc(S["s_done"], 1)

            front(0)
            for b in range(NB):
                if b + 1 < NB:
                    front(b + 1)
                if b:
                    act.wait_ge(S["x1_done"], RT * b)
                    act.wait_ge(S["at_ps"], RT * b)
                act.wait_ge(S["s_done"], RT * (b + 1))
                for r in range(RT):
                    nc.scalar.activation(A[:, r, :], sim[:, b % 2, r, :], ACT.Sigmoid, scale=SIM_SCALE).then_inc(S["sig_done"], 1)
                act.wait_ge(S["var1"], b + 1)
                nc.scalar.activation(sd[:], mv[:, :, 1], ACT.Sqrt, bias=eps_c[:]).then_inc(S["sd1"], 1)
                act.wait_ge(S["aff1"], b + 1)
                for r in range(RT):
                    nc.scalar.activation(base[:, r, :], x_sb[:, RT * b + r, :], ACT.Identity,
                                         bias=b1[:, r:r + 1], scale=s1[:, r:r + 1]).then_inc(S["base_done"], 1)
                act.wait_ge(S["var2"], b + 1)
                nc.scalar.activation(sd[:], mv[:, :, 1], ACT.Sqrt, bias=eps_c[:]).then_inc(S["sd2"], 1)
                act.wait_ge(S["aff2"], b + 1)
                if b:
                    act.wait_ge(S["xn2_out"], 16 * b)
                    act.wait_ge(S["xt_ps"], RT * b)
                for r in range(RT):
                    nc.scalar.activation(xn2[:, r, :], x1[:, r, :], ACT.Identity,
                                         bias=b2[:, r:r + 1], scale=r2[:, r:r + 1]).then_inc(S["xn2_done"], 1)
                if b:
                    act.wait_ge(S["logit_ps"], b)
                for r in range(RT):
                    act.wait_ge(S["xt_ps"], RT * b + r + 1)
                    nc.scalar.copy(xn2T[:, r, :], ps_xt).then_inc(S["xt_done"], 1)
                act.wait_ge(S["dl_done"], b + 1)
                nc.scalar.activation(ex[:], dl[:], ACT.Exp).then_inc(S["ex_done"], 1)
                for r in range(RT):
                    i = RT * b + r
                    act.wait_ge(S["scT_ps"], i + 1)
                    if i:
                        act.wait_ge(S["bd_ps"], i)
                    nc.scalar.copy(denseT[:], ps_scT).then_inc(S["scT_done"], 1)

            act.wait_ge(S["table_done"], 1)
            act.wait_ge(S["slots_done"], 1)

            def load_slots(T, k):
                off = act.value_load(tile_tab[0:1, 0, T:T + 1] if isinstance(T, int) else tile_tab[0:1, 0, bass.ds(T, 1)],
                                     min_val=0, max_val=SLOTS)
                act.dma_start(slot_sb[:, k, :], slot_d[bass.ds(off, P), :]).then_inc(slots_in[k], 16)

            def copy_xT(T, k):
                act.wait_ge(S["xT_ps"], T + 1)
                if not (isinstance(T, int) and T < 2):
                    act.wait_ge(S["gu_ps"], T - 1)
                nc.scalar.copy(xT[:, k % 2, :], ps_x[:]).then_inc(S["xT_done"], 1)

            def sigmoid(T, k):
                act.wait_ge(S["gc_done"], T + 1)
                if not (isinstance(T, int) and T == 0):
                    act.wait_ge(S["h_done"], T)
                nc.scalar.activation(sg, gc, ACT.Sigmoid, scale=ALPHA).then_inc(S["sg_done"], 1)

            def copy_hT(T, k):
                act.wait_ge(S["hT_ps"], T + 1)
                if not (isinstance(T, int) and T < 2):
                    act.wait_ge(S["y_ps"], T)
                nc.scalar.copy(hT[:, k % 2, :], ps_h[:]).then_inc(S["hT_done"], 1)

            def scale_y(T, k):
                act.wait_ge(S["y_ps"], T + 2)
                if not (isinstance(T, int) and T < 2):
                    act.wait_ge(S["added"], 16 * (T - 1))
                nc.scalar.mul(yb[:, k % 2, :], ps_y[k % 2][:],
                              slot_sb[:, k, 1:2].bitcast(fp32)).then_inc(S["y_done"], 1)

            def step(T, k):
                know = isinstance(T, int)
                if not (know and T == 0):
                    copy_hT(T - 1, (k - 1) % UNROLL)
                copy_xT(T + 1, (k + 1) % UNROLL)
                sigmoid(T, k)
                if not (know and T < 2):
                    act.wait_ge(S["added"], 16 * (T - 1))
                load_slots(T + 2, (k + 2) % UNROLL)
                if not (know and T == 0):
                    scale_y(T - 1, (k - 1) % UNROLL)

            load_slots(0, 0)
            load_slots(1, 1)
            copy_xT(0, 0)
            for T in range(UNROLL):
                step(T, T)
            with act.Fori(1, TILES // UNROLL) as lap:
                for k in range(UNROLL):
                    step(UNROLL * lap + k, k)
            copy_hT(TILES - 1, UNROLL - 1)
            scale_y(TILES - 1, UNROLL - 1)

        @block.tensor
        def _(pe):
            T_ = nc.tensor.transpose
            pe.wait_ge(S["pool_c"], 5)
            pe.wait_ge(S["const_in"], 96)
            T_(ps_k[:, 0:P], wq_sb[:], ident[:])
            T_(ps_k[:, P:2 * P], wk_sb[:], ident[:])
            for c in range(HC):
                last = T_(ps_rw[:, c * E:(c + 1) * E], rw_sb[:, c * P:(c + 1) * P], ident[0:E, 0:E])
            last.then_inc(S["wT_ps"], 1)
            pe.wait_ge(S["ctx_in_s"], 16)

            def front(b):
                if b:
                    pe.wait_ge(S["qk_done"], 2 * b)
                for r in range(RT):
                    last = T_(ps_q[:, r * P:(r + 1) * P], ctx_sb[:, b * RT + r, :], ident[:])
                last.then_inc(S["ctxT_ps"], 1)
                pe.wait_ge(S["ctxT_done"], b + 1)
                if b == 0:
                    pe.wait_ge(S["wT_done"], 3)
                nc.tensor.matmul(ps_q[:], wqT[:], ctxT[:], start=True, stop=True).then_inc(S["q_ps"], 1)
                nc.tensor.matmul(ps_k[:], wkT[:], ctxT[:], start=True, stop=True).then_inc(S["k_ps"], 1)
                pe.wait_ge(S["qk_done"], 2 * b + 2)
                for r in range(RT):
                    i = RT * b + r
                    if i >= 2:
                        pe.wait_ge(S["s_done"], i - 1)
                    nc.tensor.matmul(ps_s[i % 2][:], qT[:, r * P:(r + 1) * P], kT[:], start=True, stop=True).then_inc(S["s_ps"], 1)

            front(0)
            for b in range(NB):
                if b + 1 < NB:
                    front(b + 1)
                pe.wait_ge(S["a_done"], RT * (b + 1))
                for r in range(RT):
                    i = RT * b + r
                    if i:
                        pe.wait_ge(S["x1_done"], i)
                    for j in range(RT):
                        last = T_(ps_at[:, j * P:(j + 1) * P], A[:, j, r * P:(r + 1) * P], ident[:])
                    last.then_inc(S["at_ps"], 1)
                for r in range(RT):
                    i = RT * b + r
                    pe.wait_ge(S["xn2_done"], i + 1)
                    if i:
                        pe.wait_ge(S["xt_done"], i)
                    for c in range(HC):
                        last = T_(ps_xt[:, c * P:(c + 1) * P], xn2[:, r, c * P:(c + 1) * P], ident[:])
                    last.then_inc(S["xt_ps"], 1)
                if b:
                    pe.wait_ge(S["payload_done"], b)
                pe.wait_ge(S["xt_done"], RT * (b + 1))
                for r in range(RT):
                    for c in range(HC):
                        last = nc.tensor.matmul(ps_logit[:, r * E:(r + 1) * E], xn2T[:, r, c * P:(c + 1) * P],
                                                rwT[:, c * E:(c + 1) * E], start=(c == 0), stop=(c == HC - 1))
                last.then_inc(S["logit_ps"], 1)
                pe.wait_ge(S["hot_done"], b + 1)
                nc.tensor.matmul(ps_rank, lower[:], onehot[:].rearrange("p r e -> p (r e)"), start=True, stop=False)
                nc.tensor.matmul(ps_rank, ones[:], before[:, b * RT:(b + 1) * RT, :].rearrange("p r e -> p (r e)"),
                                 start=False, stop=True).then_inc(S["rank_ps"], 1)
                pe.wait_ge(S["dense_done"], b + 1)
                pe.wait_ge(S["payload_done"], b + 1)
                for r in range(RT):
                    i = RT * b + r
                    if i:
                        pe.wait_ge(S["scT_done"], i)
                    T_(ps_scT, dense[:, r, :], ident[:]).then_inc(S["scT_ps"], 1)
                    pe.wait_ge(S["scT_done"], i + 1)
                    if i:
                        pe.wait_ge(S["bo_done"], i)
                    nc.tensor.matmul(ps_bd, denseT[:], bd_sb[:], start=True, stop=True).then_inc(S["bd_ps"], 1)
            nc.tensor.matmul(ps_rank[:, 0:E], ones[:], before[:, NT, :], start=True, stop=True).then_inc(S["cnt_ps"], 1)

            pe.wait_ge(S["table_done"], 1)
            pe.sem_inc(S["y_ps"], 1)
            pe.wait_ge(S["bo_done"], NT)

            def tr_x(T, k):
                pe.wait_ge(S[f"gathered{k % 2}"], 8 * (T - k % 2) + 16)
                if not (isinstance(T, int) and T == 0):
                    pe.wait_ge(S["xT_done"], T)
                for c in range(HC):
                    last = T_(ps_x[:, c * P:(c + 1) * P], xg[:, k % 2, c * P:(c + 1) * P], ident[:])
                last.then_inc(S["xT_ps"], 1)

            def tr_h(T, k):
                pe.wait_ge(S["h_done"], T + 1)
                if not (isinstance(T, int) and T == 0):
                    pe.wait_ge(S["hT_done"], T)
                for c in range(HC):
                    last = T_(ps_h[:, c * P:(c + 1) * P], hb[:, k % 2, c * P:(c + 1) * P], ident[:])
                last.then_inc(S["hT_ps"], 1)

            def tab(row, T, hi):
                return pe.value_load(tile_tab[0:1, row, T:T + 1] if isinstance(T, int) else tile_tab[0:1, row, bass.ds(T, 1)],
                                     min_val=0, max_val=hi)

            def gate_up(T, k, half, buf):
                for c in range(HC):
                    last = nc.tensor.matmul(psG[k % 2][:, half * 512:(half + 1) * 512], xT[:, k % 2, c * P:(c + 1) * P],
                                            wgu[:, bass.ds(buf, 1), c, half * 512:(half + 1) * 512].rearrange("p a d -> p (a d)"),
                                            start=(c == 0), stop=(c == HC - 1))
                if half:
                    last.then_inc(S["gu_ps"], 1)

            def down(T, k, buf):
                pe.wait_ge(S["hT_done"], T + 1)
                if not (isinstance(T, int) and T < 2):
                    pe.wait_ge(S["y_done"], T - 1)
                for c in range(HC):
                    last = nc.tensor.matmul(ps_y[k % 2][:], hT[:, k % 2, c * P:(c + 1) * P],
                                            wdn[:, bass.ds(buf, 1), c, :].rearrange("p a d -> p (a d)"),
                                            start=(c == 0), stop=(c == HC - 1))
                last.then_inc(S["y_ps"], 1)

            def step(T, k):
                know = isinstance(T, int)
                buf, even, odd = tab(1, T, 1), tab(2, T, 48 * 8), tab(3, T, 48 * 8)
                pe.wait_ge(S["w0_in"], even)
                pe.wait_ge(S["w1_in"], odd)
                pe.wait_ge(S["xT_done"], T + 1)
                if not (know and T < 2):
                    pe.wait_ge(S["gu_read"], T - 1)
                gate_up(T, k, 0, buf)
                if not (know and T == 0):
                    tr_h(T - 1, (k - 1) % UNROLL)
                tr_x(T + 1, (k + 1) % UNROLL)
                gate_up(T, k, 1, buf)
                if not (know and T == 0):
                    down(T - 1, (k - 1) % UNROLL, tab(1, T - 1, 1))

            tr_x(0, 0)
            for T in range(UNROLL):
                step(T, T)
            with pe.Fori(1, TILES // UNROLL) as lap:
                for k in range(UNROLL):
                    step(UNROLL * lap + k, k)
            tr_h(TILES - 1, UNROLL - 1)
            down(TILES - 1, UNROLL - 1, tab(1, TILES - 1, 1))

        @block.vector
        def _(dve):
            n = [0]
            V = nc.vector

            def link(ins):
                n[0] += 1
                ins.then_inc(S["chain"], 1)
                dve.wait_ge(S["chain"], n[0])

            dve.wait_ge(S["pool_c"], 13)
            link(V.memset(pad_rows[:], 0))
            V.memset(zero_rows[:], 0.0).then_inc(S["dve_c"], 1)
            V.memset(eps_c[:], EPS).then_inc(S["dve_c"], 1)
            V.tensor_scalar(pad_rows[:, :, 0], pad_i[:], P - 1, TOKENS, ALU.bitwise_and, ALU.bitwise_or).then_inc(S["dve_c"], 1)
            V.memset(before[:, 0, :], 0.0).then_inc(S["dve_c"], 1)
            V.tensor_copy(payload[:, :, 0].rearrange("p (i k) -> p i k", k=TOP_K),
                          token_id[:].bitcast(u32).unsqueeze(2).broadcast_to([P, NT, TOP_K])).then_inc(S["dve_c"], 1)
            dve.wait_ge(S["wT_ps"], 1)
            V.tensor_copy(wqT[:], ps_k[:, 0:P]).then_inc(S["wT_done"], 1)
            V.tensor_copy(wkT[:], ps_k[:, P:2 * P]).then_inc(S["wT_done"], 1)
            V.tensor_copy(rwT[:], ps_rw).then_inc(S["wT_done"], 1)
            dve.wait_ge(S["gam_done"], 1)
            link(V.tensor_scalar(gam[:, 2:3], gam[:, 1:2], 0.5, None, ALU.mult))
            link(V.tensor_scalar(gam[:, 3:4], gam[:, 1:2], -1.0, 1.0, ALU.mult, ALU.add))

            for b in range(NB):
                dve.wait_ge(x_in[b], 16)
                for r in range(RT):
                    link(V.bn_stats(st[:, r, :], x_sb[:, b * RT + r, :]))
                for r in range(RT):
                    ins = V.bn_aggr(mv[:, r, :], st[:, r, :])
                    if r < RT - 1:
                        link(ins)
                ins.then_inc(S["var1"], 1)
                dve.wait_ge(S["sd1"], b + 1)
                link(V.reciprocal(rs[:], sd[:]))
                link(V.tensor_scalar(rs[:], rs[:], gam[:, 3:4], None, ALU.mult))
                link(V.tensor_tensor(b1[:], mv[:, :, 0], rs[:], ALU.mult))
                link(V.tensor_scalar(b1[:], b1[:], -1.0, None, ALU.mult))
                V.tensor_scalar(s1[:], rs[:], 1.0, None, ALU.add).then_inc(S["aff1"], 1)
                for r in range(RT):
                    dve.wait_ge(S["s_done"], RT * b + r + 1)
                    src = sim[:, b % 2, r, :]
                    for q in range((KEEP - 1) // 8):
                        link(V.max(top8[:], src if q == 0 else work[:]))
                        link(V.match_replace(work[:], top8[:], src if q == 0 else work[:], NEG))
                    link(V.max(top8[:], work[:]))
                    link(V.tensor_copy(thr[:, r:r + 1], top8[:, (KEEP - 1) % 8:(KEEP - 1) % 8 + 1]))
                dve.wait_ge(S["sig_done"], RT * (b + 1))
                for r in range(RT):
                    V.scalar_tensor_tensor(out=A[:, r, :], in0=sim[:, b % 2, r, :], scalar=thr[:, r:r + 1],
                                           in1=A[:, r, :], op0=ALU.is_ge, op1=ALU.mult).then_inc(S["a_done"], 1)
                dve.wait_ge(S["a_done"], RT * (b + 1))
                dve.wait_ge(S["base_done"], RT * (b + 1))
                for r in range(RT):
                    link(V.scalar_tensor_tensor(out=base[:, r, :], in0=A[:, r, :], scalar=gam[:, 2:3],
                                                in1=base[:, r, :], op0=ALU.mult, op1=ALU.add))
                if b:
                    dve.wait_ge(S["xn2_done"], RT * b)
                for r in range(RT):
                    dve.wait_ge(S["at_ps"], RT * b + r + 1)
                    V.scalar_tensor_tensor(out=x1[:, r, :], in0=ps_at, scalar=gam[:, 2:3],
                                           in1=base[:, r, :], op0=ALU.mult, op1=ALU.add).then_inc(S["x1_done"], 1)
                dve.wait_ge(S["x1_done"], RT * (b + 1))
                for r in range(RT):
                    link(V.bn_stats(st[:, r, :], x1[:, r, :]))
                for r in range(RT):
                    ins = V.bn_aggr(mv[:, r, :], st[:, r, :])
                    if r < RT - 1:
                        link(ins)
                ins.then_inc(S["var2"], 1)
                dve.wait_ge(S["sd2"], b + 1)
                link(V.reciprocal(r2[:], sd[:]))
                link(V.tensor_tensor(b2[:], mv[:, :, 0], r2[:], ALU.mult))
                V.tensor_scalar(b2[:], b2[:], -1.0, None, ALU.mult).then_inc(S["aff2"], 1)
                dve.wait_ge(S["logit_ps"], b + 1)
                link(V.tensor_tensor(logit[:], ps_logit.rearrange("p (r e) -> p r e", e=E),
                                     rb_sb[:].unsqueeze(1).broadcast_to([P, RT, E]), ALU.add))
                for r in range(RT):
                    link(V.max(best[:, r, :], logit[:, r, :]))
                    link(V.max_index(best_i[:, r, :], best[:, r, :], logit[:, r, :]))
                V.tensor_tensor(dl[:], best[:, :, 0:TOP_K], best[:, :, 0:1].broadcast_to([P, RT, TOP_K]),
                                ALU.subtract).then_inc(S["dl_done"], 1)
                link(V.tensor_copy(ek[:], best_i[:, :, 0:TOP_K]))
                link(V.tensor_tensor(hot[:].rearrange("p r k e -> p (r k) e"),
                                     iota_e[:].unsqueeze(1).broadcast_to([P, RT * TOP_K, E]),
                                     ek[:].rearrange("p r k -> p (r k)").unsqueeze(2).broadcast_to([P, RT * TOP_K, E]),
                                     ALU.is_equal))
                link(V.tensor_reduce(onehot[:], hot[:].rearrange("p r k e -> p r e k"), AX.X, ALU.add))
                for r in range(RT):
                    i = RT * b + r
                    ins = V.tensor_tensor(before[:, i + 1, :], before[:, i, :], onehot[:, r, :], ALU.add)
                    if r < RT - 1:
                        link(ins)
                ins.then_inc(S["hot_done"], 1)
                dve.wait_ge(S["ex_done"], b + 1)
                link(V.tensor_reduce(den[:], ex[:], AX.X, ALU.add))
                link(V.reciprocal(den[:], den[:]))
                link(V.tensor_tensor(score[:], ex[:], den[:].unsqueeze(2).broadcast_to([P, RT, TOP_K]), ALU.mult))
                link(V.tensor_tensor(hotv[:].rearrange("p r k e -> p (r k) e"), hot[:].rearrange("p r k e -> p (r k) e"),
                                     score[:].rearrange("p r k -> p (r k)").unsqueeze(2).broadcast_to([P, RT * TOP_K, E]),
                                     ALU.mult))
                V.tensor_reduce(dense[:], hotv[:].rearrange("p r k e -> p r e k"), AX.X, ALU.add).then_inc(S["dense_done"], 1)
                dve.wait_ge(S["dense_done"], b + 1)
                dve.wait_ge(S["rank_ps"], b + 1)
                link(V.tensor_tensor(pos[:], ps_rank.rearrange("p (r e) -> p r e", e=E),
                                     slot0_e[:].unsqueeze(1).broadcast_to([P, RT, E]), ALU.add))
                for r in range(RT):
                    link(V.tensor_tensor(hotv[:, r], hot[:, r], pos[:, r, :].unsqueeze(1).broadcast_to([P, TOP_K, E]), ALU.mult))
                link(V.tensor_reduce(posk[:], hotv[:], AX.X, ALU.add))
                sl = slice(b * RT * TOP_K, (b + 1) * RT * TOP_K)
                link(V.tensor_copy(slot_i[:, sl], posk[:].rearrange("p r k -> p (r k)")))
                V.tensor_copy(payload[:, sl, 1].bitcast(fp32), score[:].rearrange("p r k -> p (r k)")).then_inc(S["payload_done"], 1)
                if b:
                    dve.wait_ge(S["acc_out"], 16 * b)
                for r in range(RT):
                    i = RT * b + r
                    dve.wait_ge(S["bd_ps"], i + 1)
                    V.tensor_tensor(base_out[:, r, :], ps_bd, x1[:, r, :], ALU.add).then_inc(S["bo_done"], 1)

            dve.wait_ge(S["cnt_ps"], 1)
            link(V.tensor_copy(cnt[:], ps_rank[0:1, 0:E]))
            link(V.tensor_tensor(ncmp[:], cnt[:].unsqueeze(2).broadcast_to([1, E, E]),
                                 jtab[:].unsqueeze(1).broadcast_to([1, E, E]), ALU.is_gt))
            link(V.tensor_reduce(til[:], ncmp[:], AX.X, ALU.add))
            link(V.tensor_copy(cum[:, 0, :], til[:]))
            src = 0
            for s in (1, 2, 4, 8):
                link(V.tensor_tensor(cum[:, 1 - src, s:E], cum[:, src, s:E], cum[:, src, 0:E - s], ALU.add))
                link(V.tensor_copy(cum[:, 1 - src, 0:s], cum[:, src, 0:s]))
                src = 1 - src
            link(V.tensor_copy(end_tab[:], cum[:, src, :]))
            link(V.tensor_tensor(cmp_t[:], ttab[:].unsqueeze(2).broadcast_to([1, TABLE, E]),
                                 cum[:, src, :].unsqueeze(1).broadcast_to([1, TABLE, E]), ALU.is_ge))
            link(V.tensor_reduce(tf[:, 0, :], cmp_t[:], AX.X, ALU.add))
            link(V.tensor_tensor(cmp_w[:], cmp_t[:], til[:].unsqueeze(1).broadcast_to([1, TABLE, E]), ALU.mult))
            link(V.tensor_reduce(tf[:, 1, :], cmp_w[:], AX.X, ALU.add))
            link(V.tensor_tensor(cmp_w[:], cmp_t[:], alt[:].unsqueeze(1).broadcast_to([1, TABLE, E]), ALU.mult))
            link(V.tensor_reduce(tf[:, 2, :], cmp_w[:], AX.X, ALU.add))
            link(V.tensor_tensor(tf[:, 3, :], ttab[:], tf[:, 1, :], ALU.subtract))
            link(V.tensor_scalar(tf[:, 3, :], tf[:, 3, :], float(P), None, ALU.mult))
            link(V.scalar_tensor_tensor(out=tf[:, 3, :], in0=tf[:, 0, :], scalar=float(TOKENS), in1=tf[:, 3, :],
                                        op0=ALU.mult, op1=ALU.add))
            link(V.tensor_scalar(tf[:, 3, :], tf[:, 3, :], float(SLOTS), None, ALU.min))
            link(V.tensor_scalar(tf[:, 0, :], tf[:, 0, :], float(E - 1), None, ALU.min))
            link(V.tensor_tensor(tf[:, 4, :], tf[:, 0, :], tf[:, 2, :], ALU.subtract))
            link(V.tensor_scalar(tf[:, 4, :], tf[:, 4, :], 2.0, 24.0, ALU.add, ALU.mult))
            link(V.tensor_scalar(tf[:, 4, :], tf[:, 4, :], float(48 * E // 2), None, ALU.min))
            link(V.tensor_tensor(tf[:, 5, :], tf[:, 0, :], tf[:, 2, :], ALU.add))
            link(V.tensor_scalar(tf[:, 5, :], tf[:, 5, :], 24.0, 48.0, ALU.mult, ALU.max))
            link(V.tensor_copy(tile_tab[:, 0, :], tf[:, 3, :]))
            link(V.tensor_copy(tile_tab[:, 1, :], tf[:, 2, :]))
            link(V.tensor_copy(tile_tab[:, 2, :], tf[:, 4, :]))
            V.tensor_copy(tile_tab[:, 3, :], tf[:, 5, :]).then_inc(S["table_done"], 1)
            dve.wait_ge(S["table_done"], 1)

            c0 = n[0]

            def step(T, k):
                know = isinstance(T, int)
                buf = dve.value_load(tile_tab[0:1, 1, T:T + 1] if know else tile_tab[0:1, 1, bass.ds(T, 1)],
                                     min_val=0, max_val=1)
                dve.wait_ge(S["gu_ps"], T + 1)
                V.tensor_tensor(gu, psG[k % 2][:], bgu[:, bass.ds(buf, 1), :].rearrange("p a d -> p (a d)"),
                                ALU.add).then_inc(S["gu_read"], 1)
                dve.wait_ge(S["gu_read"], T + 1)
                gv = gu.rearrange("p (d t) -> p t d", t=2)
                V.tensor_scalar(gc, gv[:, 0, :], LIMIT, None, ALU.min).then_inc(S["gc_done"], 1)
                V.tensor_scalar(uc, gv[:, 1, :], LIMIT, -LIMIT, ALU.min, ALU.max).then_inc(S["chain"], 1)
                dve.wait_ge(S["chain"], 2 * T + (c0 + 1))
                dve.wait_ge(S["gc_done"], T + 1)
                V.scalar_tensor_tensor(out=h1, in0=uc, scalar=1.0, in1=gc, op0=ALU.add, op1=ALU.mult).then_inc(S["chain"], 1)
                dve.wait_ge(S["chain"], 2 * T + (c0 + 2))
                dve.wait_ge(S["sg_done"], T + 1)
                if not (know and T < 2):
                    dve.wait_ge(S["hT_ps"], T - 1)
                V.tensor_tensor(hb[:, k % 2, :], h1, sg, ALU.mult).then_inc(S["h_done"], 1)

            for T in range(UNROLL):
                step(T, T)
            with dve.Fori(1, TILES // UNROLL) as lap:
                for k in range(UNROLL):
                    step(UNROLL * lap + k, k)


_INS = ["x", "ctx_512", "L0_xattn_Wq", "L0_xattn_Wk", "L0_xattn_gamma_raw", "L0_ffn_router_weight",
        "L0_ffn_router_bias", "L0_ffn_gate_up_proj", "L0_ffn_gate_up_proj_bias", "L0_ffn_down_proj",
        "L0_ffn_down_proj_bias"]
_OUTS = [((4, 512, 512), "float32")]


def kernel(**inputs):
    import numpy as _np
    import concourse.bacc as _bacc
    from concourse import mybir as _mybir
    from concourse.bass_utils import run_bass_kernel_spmd as _run

    nc = _bacc.Bacc("TRN2", target_bir_lowering=False, num_devices=1)
    arrays, args = {}, []
    for name in _INS:
        a = _np.ascontiguousarray(_np.atleast_1d(_np.asarray(inputs[name])))
        arrays[f"in_{name}_dram"] = a
        args.append(nc.dram_tensor(f"in_{name}_dram", a.shape, _mybir.dt.from_np(a.dtype), kind="ExternalInput").ap())
    for i, (shape, dtype) in enumerate(_OUTS):
        dt = _mybir.dt.from_np(_np.dtype(dtype))
        args.append(nc.dram_tensor(f"out_{i}_dram", shape, dt, kind="ExternalOutput").ap())
    xattn_moe_kernel(nc, *args)
    r = _run(nc, [arrays], core_ids=[0])
    return r.results[0]["out_0_dram"]
```

```python
import concourse.bass as bass
from concourse import mybir
from contextlib import ExitStack

P = 128
NB, N, H = 4, 512, 512
C = 128
HEADS = 4
E, TOP_K, D = 16, 4, 512
RT = N // P
NT = NB * RT
TOKENS = NB * N
HC = H // P
KEEP = max(1, int(N * 0.3))
SIM_SCALE = 1.0 / ((C // HEADS) ** 0.5 * HEADS)
ALPHA, LIMIT = 1.702, 7.0
EPS = 1e-5
NEG = -3.0e38
GAINS = (0.8, 0.7, 0.6, 0.5, 0.4, 0.3)
QUANTILE, DENSITY = 0.54, 0.345
AIM = KEEP - 4.5
BIG = 2.0 ** 100
UNROLL = 4
TILES = -(-(TOKENS * TOP_K // P + E - 1) // UNROLL) * UNROLL
SLOTS = E * TOKENS
GU = 2 * D
WIDE = GU + H
TABLE = TILES + 4
LAPS = TILES // UNROLL
FIELDS = {"buffer": (0, 1, 1), "some": (1, 1, 1), "more": (2, 1, 1), "first": (3, 2, HC - 1), "end": (5, 3, HC),
          "split": (8, 7, HC * E), "start": (15, 7, TILES), "buffer_before": (22, 1, 1),
          "slots_1": (0, 9, SLOTS // P), "slots_3": (9, 9, SLOTS // P)}
AT_ONCE = 2


def xattn_moe_kernel(nc, x, ctx_in, wq, wk, gamma_raw, rw, rb, gup, gupb, dwn, dwnb, out):
    f32r = mybir.dt.float32r
    fp32, u32, i32 = mybir.dt.float32, mybir.dt.uint32, mybir.dt.int32
    ALU = mybir.AluOpType
    ACT = mybir.ActivationFunctionType
    AX = mybir.AxisListType

    x_v = x.rearrange("b (r p) h -> p (b r) h", p=P)
    ctx_v = ctx_in.rearrange("b (r p) c -> p (b r) c", p=P)
    out_v = out.rearrange("b n h -> (b n) h")
    gup_v = gup.rearrange("e (c p) d -> e p c d", p=P)
    dwn_v = dwn.rearrange("e (c p) h -> e p c h", p=P)

    xn_d = nc.dram_tensor("xn_rows", [TOKENS + P, H], fp32, kind="Internal").ap()
    acc_d = nc.dram_tensor("acc_rows", [TOKENS + P, H], fp32, kind="Internal").ap()
    slot_d = nc.dram_tensor("slot_rows", [SLOTS + P, 2], u32, kind="Internal").ap()

    ctx = ExitStack()
    with ctx:
        def sb(name, shape, dt=fp32):
            return ctx.enter_context(nc.sbuf_tensor(name, shape, dt))

        def sem(name):
            return ctx.enter_context(nc.semaphore(name))

        banks = [ctx.enter_context(nc.psum_tensor(f"bank{i}", [P, 512], fp32)) for i in range(2)]
        bank67 = [ctx.enter_context(nc.psum_tensor(f"bank{i}", [P, 512], fp32)) for i in range(2, 4)]
        psG = [ctx.enter_context(nc.psum_tensor(f"gate_up_ps{i}", [P, GU], fp32)) for i in range(2)]
        ps_q, ps_k = banks
        ps_s = bank67
        ps_t = [psG[0][:, 0:512], psG[0][:, 512:1024]]
        ps_bd = [psG[1][:, 0:512], psG[0][:, 512:1024]]
        ps_m = psG[1][:, 512:1024]
        ps_logit = ps_m[:, 0:RT * E]
        ps_rank = ps_m[:, 64:64 + RT * E]
        ps_rw = ps_m[:, 128:128 + HC * E]
        ps_ok = ps_m[:, 256:256 + RT]
        ps_scT = ps_t[0][0:E, :]
        ps_x, ps_h = banks
        ps_y = bank67

        raw_w = sb("raw_w", [P, HC, WIDE])
        raw_b = sb("raw_b", [P, HC, GU // HC])
        bgu = sb("bgu", [P, 2, GU])
        gslot = sb("gslot", [P, UNROLL, 2], u32)
        aslot = sb("aslot", [P, UNROLL, 2], u32)
        ident = sb("ident", [P, P])
        tile_tab = sb("tile_tab", [1, 2, TABLE], i32)
        laps_tab = sb("laps_tab", [1, 1], i32)
        slot_i = sb("slot_i", [P, NT * TOP_K], u32)
        payload = sb("payload", [P, NT * TOP_K, 2], u32)
        at = -(-nc.sbuf_base // 64) * 64
        half_bytes = 2 * HC * WIDE * 4
        w = nc.alloc_sbuf_tensor_at("w", [P, 2, 2, HC, WIDE], f32r, offset=at)
        even_half = sb("even_half", [P, half_bytes // 4 + 16])
        free = [at + 2 * half_bytes]

        def tile_sb(name, shape, dt=fp32):
            n = 4
            for d in shape[1:]:
                n *= d
            t = nc.alloc_sbuf_tensor_at(name, shape, dt, offset=free[0])
            free[0] += -(-n // 64) * 64
            return t

        xg = tile_sb("xg", [P, UNROLL, H])
        xh, xl = tile_sb("xh", [P, 2, H], f32r), tile_sb("xl", [P, 2, H], f32r)
        gu = tile_sb("gu", [P, GU])
        gc, uc = tile_sb("gc", [P, D]), tile_sb("uc", [P, D])
        sg, h1 = tile_sb("sg", [P, D]), tile_sb("h1", [P, D])
        hb = tile_sb("hb", [P, 2, D])
        hh, hl = tile_sb("hh", [P, 2, D], f32r), tile_sb("hl", [P, 2, D], f32r)
        yb = tile_sb("yb", [P, 2, H])

        x_sb = sb("x_sb", [P, NT, H])
        ctx_sb = sb("ctx_sb", [P, NT, C])
        wq_sb, wk_sb = sb("wq_sb", [P, C]), sb("wk_sb", [P, C])
        wqT, wkT = sb("wqT", [P, C]), sb("wkT", [P, C])
        rw_sb = sb("rw_sb", [E, H])
        rwT = sb("rwT", [P, HC * E])
        rb_sb = sb("rb_sb", [P, E])
        bd_sb = sb("bd_sb", [E, H])
        lower = sb("lower", [P, P])
        ones = sb("ones", [P, P])
        iota_e = sb("iota_e", [P, E])
        slot0_e = sb("slot0_e", [P, E])
        token_id = sb("token_id", [P, NT], i32)
        gam = sb("gam", [P, 4])
        eps_c = sb("eps_c", [P, 1])
        ctxT, qT, kT = sb("ctxT", [P, N]), sb("qT", [P, N]), sb("kT", [P, N])
        sim = sb("sim", [P, 2, RT, N])
        work = sb("work", [P, N])
        marks = sb("marks", [P, N])
        junk = sb("junk", [P, RT, N], mybir.dt.bfloat16)
        minus_big = sb("minus_big", [P, 1])
        iota8 = sb("iota8", [P, 8])
        top8 = sb("top8", [P, RT, 8])
        pick = sb("pick", [P, RT, 8])
        above = sb("above", [P, RT])
        okv = sb("okv", [P, RT])
        okf = sb("okf", [P, 1])
        oki = sb("oki", [P, 1], i32)
        guess = sb("guess", [P, RT])
        nguess = sb("nguess", [P, 2, RT])
        slope = sb("slope", [P, 2, RT])
        signs = sb("signs", [P, 2, RT])
        step_u = sb("step_u", [P, 2, RT])
        st1 = sb("st1", [P, 2, RT, 6])
        mv1 = sb("mv1", [P, 2, RT, 2])
        sd1 = sb("sd1", [P, 2, RT])
        thr = sb("thr", [P, RT])
        A = sb("A", [P, RT, N])
        pads = (SLOTS + P) // P
        pad_i = A[:, 0, 0:pads].bitcast(i32)
        pad_rows = A[:].rearrange("p r n -> p (r n)")[:, N:N + 2 * pads].bitcast(i32).rearrange("p (a t) -> p a t", t=2)
        zero_rows = A[:, 3, :]
        x1 = sb("x1", [P, RT, N])
        xn2 = sb("xn2", [P, RT, N])
        xn2T = sb("xn2T", [P, RT, N])
        st = sb("st", [P, RT, 6])
        mv = sb("mv", [P, RT, 2])
        sd = sb("sd", [P, RT])
        rs = sb("rs", [P, RT])
        s1, b1 = sb("s1", [P, 2, RT]), sb("b1", [P, 2, RT])
        r2, b2 = sb("r2", [P, RT]), sb("b2", [P, RT])
        logit = sb("logit", [P, RT, E])
        best = sb("best", [P, RT, 8])
        best_i = sb("best_i", [P, RT, 8], u32)
        ek = sb("ek", [P, RT, TOP_K])
        dl = sb("dl", [P, RT, TOP_K])
        ex = sb("ex", [P, RT, TOP_K])
        den = sb("den", [P, RT])
        score = sb("score", [P, RT, TOP_K])
        hot = sb("hot", [P, RT, TOP_K, E])
        hotv = sb("hotv", [P, RT, TOP_K, E])
        onehot = sb("onehot", [P, RT, E])
        before = sb("before", [P, NT + 1, E])
        dense = sb("dense", [P, RT, E])
        denseT = sb("denseT", [E, RT * P])
        pos = sb("pos", [P, RT, E])
        posk = sb("posk", [P, RT, TOP_K])
        base_out = x1
        cnt = sb("cnt", [1, E])
        jtab = sb("jtab", [1, E])
        til = sb("til", [1, E])
        cum = sb("cum", [1, 2, E])
        ttab = sb("ttab", [1, TABLE])
        alt = sb("alt", [1, E])
        flat_a, flat_x = A[0:1].rearrange("p r n -> p (r n)"), xn2T[0:1].rearrange("p r n -> p (r n)")
        cmp_t = flat_a[:, 0:TABLE * E].rearrange("p (t e) -> p t e", e=E)
        tf = flat_a[:, TABLE * E:TABLE * (E + 8)].rearrange("p (w t) -> p w t", w=8)
        cmp_w = flat_x[:, 0:TABLE * E].rearrange("p (t e) -> p t e", e=E)
        more_f = flat_x[:, TABLE * E + E * E:TABLE * (E + 1) + E * E]
        word_f = flat_x[:, TABLE * (E + 1) + E * E:TABLE * (E + 3) + E * E].rearrange("p (w t) -> p w t", w=2)
        ncmp = flat_x[:, TABLE * E:TABLE * E + E * E].rearrange("p (t e) -> p t e", e=E)
        lapj = sb("lapj", [1, LAPS])
        S = {}
        for name in ("const_in", "ctx_in_s", "bias_in", "pad_out", "pool_c", "dve_c", "wT_ps", "wT_done", "gam_done",
                     "ctxT_ps", "ctxT_done", "q_ps", "k_ps", "qk_done", "s_ps", "s_done", "sig_done",
                     "a_done", "at_ps", "x1_done", "var1", "sd1", "aff1", "base_done", "var2", "sd2", "aff2",
                     "xn2_done", "xn2_out", "xt_ps", "xt_done", "logit_ps", "dl_done", "ex_done", "hot_done",
                     "rank_ps", "dense_done", "scT_ps", "scT_done", "bd_ps", "bo_done", "acc_out", "slots_done",
                     "payload_done", "scat", "chain", "cnt_ps", "table_done", "guess_done", "counted", "moved", "ok_done", "ok_ps",
                     "raw_in", "hi_done", "lo_done", "xT_ps", "xh_done", "xl_done", "gu_ps", "gu_read", "gc_done", "sg_done",
                     "h_done", "hT_ps", "hh_done", "hl_done", "y_ps", "y_done", "added",
                     "fin", "all_added", "achain", "pchain", "turn"):
            S[name] = sem(name)
        x_in = [sem(f"x_in{b}") for b in range(NB)]
        gslot_in = [sem(f"gslot_in{k}") for k in range(UNROLL)]
        aslot_in = [sem(f"aslot_in{k}") for k in range(UNROLL)]
        gathered = [sem(f"gathered{k}") for k in range(UNROLL)]

        def known(T, below=1):
            return isinstance(T, int) and T < below

        def word(eng, row, T):
            cell = tile_tab[0:1, row, T:T + 1] if isinstance(T, int) else tile_tab[0:1, row, bass.ds(T, 1)]
            return eng.value_load(cell, min_val=0, max_val=(1 << 24) - 1)

        def field(eng, value, name):
            at_bit, bits, most = FIELDS[name]
            return nc.s_assert_within(eng.snap((value >> at_bit) & ((1 << bits) - 1)), 0, most,
                                      skip_runtime_bounds_check_because="the table is built within these bounds")

        def final_lap(eng):
            return eng.value_load(laps_tab[0:1, 0:1], min_val=TOKENS * TOP_K // P // UNROLL - 1, max_val=LAPS - 1)

        def slot_count(T, k):
            return 16 * ((T - k) // UNROLL + 1) if isinstance(T, int) else 4 * (T - k) + 16

        block = ctx.enter_context(nc.Block())

        @block.sync
        def _(sp):
            sp.dma_start(ctx_sb[:], ctx_v).then_inc(S["ctx_in_s"], 16)
            sp.dma_start(wq_sb[:], wq).then_inc(S["const_in"], 16)
            sp.dma_start(wk_sb[:], wk).then_inc(S["const_in"], 16)
            sp.dma_start(rw_sb[:], rw).then_inc(S["const_in"], 16)
            sp.dma_start(bd_sb[:], dwnb).then_inc(S["const_in"], 16)
            sp.dma_start(rb_sb[:], rb.rearrange("(a e) -> a e", a=1).broadcast_to([P, E])).then_inc(S["const_in"], 16)
            sp.dma_start(gam[:, 0:1], gamma_raw.rearrange("(a e) -> a e", a=1).broadcast_to([P, 1])).then_inc(S["const_in"], 16)
            for b in range(NB):
                sp.dma_start(x_sb[:, b * RT:(b + 1) * RT, :], x_v[:, b * RT:(b + 1) * RT, :]).then_inc(x_in[b], 16)
            sp.wait_ge(S["dve_c"], 3)
            sp.dma_start(slot_d.rearrange("(p a) t -> p a t", p=P), pad_rows.bitcast(u32)).then_inc(S["pad_out"], 16)
            sp.dma_start(xn_d[TOKENS:TOKENS + P, :], zero_rows).then_inc(S["pad_out"], 16)
            sp.dma_start(acc_d[TOKENS:TOKENS + P, :], zero_rows).then_inc(S["pad_out"], 16)

            def load_expert(e):
                gate_up, down, bias = (gup_v[e], dwn_v[e], gupb[e:e + 1, :]) if isinstance(e, int) else (
                    gup_v[bass.ds(e, 1)].rearrange("a p c d -> p (a c) d"),
                    dwn_v[bass.ds(e, 1)].rearrange("a p c d -> p (a c) d"), gupb[bass.ds(e, 1), :])
                sp.dma_start(raw_w[:, :, 0:GU], gate_up).then_inc(S["raw_in"], 16)
                sp.dma_start(raw_w[:, :, GU:WIDE], down).then_inc(S["raw_in"], 16)
                sp.dma_start(raw_b[:].rearrange("p c d -> p (c d)"), bias.broadcast_to([P, GU])).then_inc(S["raw_in"], 16)

            load_expert(0)
            for b in range(NB):
                rows = slice(b * N, (b + 1) * N)
                if b == NB - 1:
                    sp.wait_ge(S["lo_done"], HC)
                    load_expert(1)
                sp.wait_ge(S["xn2_done"], RT * (b + 1))
                sp.dma_start(xn_d[rows, :].rearrange("(r p) h -> p r h", p=P), xn2[:]).then_inc(S["xn2_out"], 16)
                sp.wait_ge(S["bo_done"], RT * (b + 1))
                sp.dma_start(acc_d[rows, :].rearrange("(r p) h -> p r h", p=P), base_out[:]).then_inc(S["acc_out"], 16)
            with sp.Fori(2, E) as e:
                sp.wait_ge(S["lo_done"], HC * e)
                load_expert(e)
            sp.wait_ge(S["all_added"], 1)
            sp.dma_start(out_v, acc_d[0:TOKENS, :]).then_inc(S["fin"], 16)
            sp.wait_ge(S["fin"], 16)

        @block.gpsimd
        def _(pool):
            c = S["pool_c"]
            pool.memset(ident[:], 0.0).then_inc(c, 1)
            pool.memset(lower[:], 1.0).then_inc(c, 1)
            pool.memset(ones[:], 1.0).then_inc(c, 1)
            pool.wait_ge(c, 3)
            pool.affine_select(out=ident[:], in_=ident[:], compare_op=ALU.not_equal, fill=1.0, base=0,
                               pattern=[[-1, P]], channel_multiplier=1).then_inc(c, 1)
            pool.affine_select(out=lower[:], in_=lower[:], compare_op=ALU.is_gt, fill=0.0, base=0,
                               pattern=[[1, P]], channel_multiplier=-1).then_inc(c, 1)
            kw = dict(allow_small_or_imprecise_dtypes=True)
            pool.iota(iota_e[:], pattern=[[1, E]], base=0, channel_multiplier=0, **kw).then_inc(c, 1)
            pool.iota(slot0_e[:], pattern=[[TOKENS, E]], base=0, channel_multiplier=0, **kw).then_inc(c, 1)
            pool.iota(token_id[:], pattern=[[P, NT]], base=0, channel_multiplier=1).then_inc(c, 1)
            pool.iota(pad_i, pattern=[[1, (SLOTS + P) // P]], base=0, channel_multiplier=1).then_inc(c, 1)
            pool.iota(jtab[:], pattern=[[P, E]], base=0, channel_multiplier=0, **kw).then_inc(c, 1)
            pool.iota(ttab[:], pattern=[[1, TABLE]], base=0, channel_multiplier=0, **kw).then_inc(c, 1)
            pool.memset(alt[:], -1.0).then_inc(c, 1)
            pool.iota(lapj[:], pattern=[[UNROLL, LAPS]], base=0, channel_multiplier=0, **kw).then_inc(c, 1)
            pool.iota(iota8[:], pattern=[[1, 8]], base=0, channel_multiplier=0, **kw).then_inc(c, 1)
            pool.wait_ge(c, 12)
            pool.memset(alt[:, 0:E:2], 1.0).then_inc(c, 1)
            n = [0]

            def link(ins):
                n[0] += 1
                ins.then_inc(S["pchain"], 1)
                pool.wait_ge(S["pchain"], n[0])

            scattered = [0]

            def scatter(batches, count):
                for k in range(scattered[0], min(scattered[0] + count, batches * RT * TOP_K)):
                    if k == 0:
                        pool.wait_ge(S["pad_out"], 48)
                    if k % (RT * TOP_K) == 0:
                        pool.wait_ge(S["payload_done"], k // (RT * TOP_K) + 1)
                    pool.indirect_dma_start(slot_d, bass.IndirectOffsetOnAxis(slot_i[:, k:k + 1], 0),
                                            payload[:, k, :], None).then_inc(S["scat"], 16)
                    scattered[0] += 1

            for b in range(NB):
                for it, gain in enumerate(GAINS):
                    for h in range(2):
                        rr = slice(2 * h, 2 * h + 2)
                        pool.wait_ge(S["counted"], RT * (len(GAINS) * b + it) + 2 * h + 2)
                        link(pool.tensor_scalar(step_u[:, h, 0:2], signs[:, b % 2, rr], float(N - 2 * AIM),
                                                -gain / 2, ALU.add, ALU.mult))
                        link(pool.tensor_tensor(step_u[:, h, 2:4], step_u[:, h, 0:2], slope[:, b % 2, rr], ALU.mult))
                        pool.tensor_tensor(nguess[:, b % 2, rr], nguess[:, b % 2, rr], step_u[:, h, 2:4],
                                           ALU.add).then_inc(S["moved"], 1)
                        if b >= 2:
                            scatter(b - 1, 1)
                pool.wait_ge(S["raw_in"], 48)
                pool.tensor_copy(w[:, 0, 0, b, :], raw_w[:, b, :]).then_inc(S["hi_done"], 1)
                pool.tensor_copy(bgu[:, 0, b * (GU // HC):(b + 1) * (GU // HC)], raw_b[:, b, :])
                pool.wait_ge(S["hi_done"], b + 1)
                pool.tensor_tensor(w[:, 0, 1, b, :], raw_w[:, b, :], w[:, 0, 0, b, :].bitcast(fp32),
                                   ALU.subtract).then_inc(S["lo_done"], 1)
            scatter(NB, NT * TOP_K)
            pool.wait_ge(S["scat"], 16 * NT * TOP_K)
            pool.sem_inc(S["slots_done"], 1)
            pool.wait_ge(S["xn2_out"], 16 * NB)
            pool.wait_ge(S["acc_out"], 16 * NB)

            def gather(T, k):
                pool.wait_ge(gslot_in[k], slot_count(T, k))
                if not known(T, UNROLL):
                    pool.wait_ge(S["xT_ps"], T - UNROLL + 1)
                pool.sem_inc(S["turn"], 1)
                pool.indirect_dma_start(xg[:, k, :], None, xn_d,
                                        bass.IndirectOffsetOnAxis(gslot[:, k, 0:1], 0)).then_inc(gathered[k], 16)

            def add(T, k):
                pool.wait_ge(S["y_done"], T + 1)
                if not known(T):
                    pool.wait_ge(S["added"], 16 * T)
                pool.sem_inc(S["turn"], 1)
                pool.indirect_dma_start(acc_d, bass.IndirectOffsetOnAxis(aslot[:, k, 0:1], 0),
                                        yb[:, k % 2, :], None, compute_op=ALU.add).then_inc(S["added"], 16)

            def step(T, k):
                gather(T + 2, (k + 2) % UNROLL)
                if not known(T):
                    add(T - 1, (k - 1) % UNROLL)

            gather(0, 0)
            pool.wait_ge(S["table_done"], 1)
            final = final_lap(pool)
            gather(1, 1)
            for T in range(UNROLL):
                step(T, T)
            with pool.Fori(1, final + 1) as lap:
                for k in range(UNROLL):
                    step(UNROLL * lap + k, k)
            add(UNROLL * final + (UNROLL - 1), UNROLL - 1)
            pool.wait_ge(S["added"], 16 * UNROLL * final + 16 * UNROLL)
            pool.sem_inc(S["all_added"], 1)
            for k in range(2):
                pool.wait_ge(gathered[k], 16 * final + 32)
            pool.wait_ge(aslot_in[0], 16 * final + 32)
            pool.wait_ge(gslot_in[2], 16 * final + 32)
            pool.sem_inc(S["turn"], 1)

        @block.scalar
        def _(act):
            n = [0]

            def link(ins):
                n[0] += 1
                ins.then_inc(S["achain"], 1)
                act.wait_ge(S["achain"], n[0])

            act.wait_ge(S["const_in"], 96)
            nc.scalar.activation(gam[:, 1:2], gam[:, 0:1], ACT.Sigmoid).then_inc(S["gam_done"], 1)

            def project(b):
                act.wait_ge(S["ctxT_ps"], b + 1)
                if b:
                    act.wait_ge(S["k_ps"], b)
                nc.scalar.copy(ctxT[:], ps_q[:]).then_inc(S["ctxT_done"], 1)
                if b:
                    act.wait_ge(S["s_ps"], RT * b)
                act.wait_ge(S["q_ps"], b + 1)
                nc.scalar.copy(qT[:], ps_q[:]).then_inc(S["qk_done"], 1)
                act.wait_ge(S["k_ps"], b + 1)
                nc.scalar.copy(kT[:], ps_k[:]).then_inc(S["qk_done"], 1)

            def scores(b):
                for r in range(RT):
                    i = RT * b + r
                    act.wait_ge(S["s_ps"], i + 1)
                    if b >= 2:
                        act.wait_ge(S["a_done"], RT * (b - 1))
                    nc.scalar.copy(sim[:, b % 2, r, :], ps_s[i % 2][:]).then_inc(S["s_done"], 1)

            def deviations(b):
                act.wait_ge(S["var1"], b + 1)
                nc.scalar.activation(sd1[:], mv1[:, :, :, 1], ACT.Sqrt, bias=eps_c[:]).then_inc(S["sd1"], 1)

            def search(b):
                act.wait_ge(S["guess_done"], b + 1)
                if b:
                    act.wait_ge(S["counted"], RT * len(GAINS) * b)
                for it in range(len(GAINS)):
                    for r in range(RT):
                        if it and r % 2 == 0:
                            act.wait_ge(S["moved"], 2 * (len(GAINS) * b + it - 1) + r // 2 + 1)
                        nc.scalar.activation(junk[:, r, :], sim[:, b % 2, r, :], ACT.Sign, bias=nguess[:, b % 2, r:r + 1],
                                             accum_out=signs[:, b % 2, r:r + 1]).then_inc(S["counted"], 1)

            def gates(b):
                if b:
                    act.wait_ge(S["x1_done"], RT * b)
                    act.wait_ge(S["at_ps"], RT * b)
                else:
                    act.wait_ge(S["pad_out"], 48)
                for r in range(RT):
                    nc.scalar.activation(A[:, r, :], sim[:, b % 2, r, :], ACT.Sigmoid, scale=SIM_SCALE).then_inc(S["sig_done"], 1)
                act.wait_ge(S["aff1"], b + 1)
                for r in range(RT):
                    nc.scalar.activation(x_sb[:, RT * b + r, :], x_sb[:, RT * b + r, :], ACT.Identity,
                                         bias=b1[:, b % 2, r:r + 1], scale=s1[:, b % 2, r:r + 1]).then_inc(S["base_done"], 1)

            def norm(b):
                act.wait_ge(S["var2"], b + 1)
                nc.scalar.activation(sd[:], mv[:, :, 1], ACT.Sqrt, bias=eps_c[:]).then_inc(S["sd2"], 1)
                act.wait_ge(S["aff2"], b + 1)
                if b:
                    act.wait_ge(S["xn2_out"], 16 * b)
                    act.wait_ge(S["xt_ps"], RT * b)
                for r in range(RT):
                    nc.scalar.activation(xn2[:, r, :], x1[:, r, :], ACT.Identity,
                                         bias=b2[:, r:r + 1], scale=r2[:, r:r + 1]).then_inc(S["xn2_done"], 1)
                if b:
                    act.wait_ge(S["logit_ps"], b)
                for r in range(RT):
                    act.wait_ge(S["xt_ps"], RT * b + r + 1)
                    nc.scalar.copy(xn2T[:, r, :], ps_t[r % 2]).then_inc(S["xt_done"], 1)

            def exponentials(b):
                act.wait_ge(S["dl_done"], b + 1)
                nc.scalar.activation(ex[:], dl[:], ACT.Exp).then_inc(S["ex_done"], 1)

            def routed(b):
                act.wait_ge(S["scT_ps"], b + 1)
                if b:
                    act.wait_ge(S["bd_ps"], RT * b)
                nc.scalar.copy(denseT[:], ps_scT).then_inc(S["scT_done"], 1)

            project(0)
            scores(0)
            deviations(0)
            search(0)
            deviations(1)
            gates(0)
            for b in range(NB):
                if b + 1 < NB:
                    search(b + 1)
                norm(b)
                if b + 1 < NB:
                    gates(b + 1)
                if b + 2 < NB:
                    project(b + 2)
                exponentials(b)
                if b + 2 < NB:
                    scores(b + 2)
                routed(b)
                if b + 2 < NB:
                    deviations(b + 2)

            act.wait_ge(S["slots_done"], 1)
            act.wait_ge(S["acc_out"], 16 * NB)
            act.wait_ge(S["xn2_out"], 16 * NB)
            act.wait_ge(S["bo_done"], NT)

            def load_slots(tile, k, buf, done):
                act.dma_start(buf[:, k, :], slot_d[bass.ds(tile * P, P), :]).then_inc(done[k], 16)

            def high_x(T, k):
                act.wait_ge(S["xT_ps"], T + 1)
                if not known(T, 2):
                    act.wait_ge(S["gu_ps"], T - 1)
                nc.scalar.copy(xh[:, k % 2, :], ps_x[:]).then_inc(S["xh_done"], 1)

            def high_h(T, k):
                act.wait_ge(S["hT_ps"], T + 1)
                if not known(T, 2):
                    act.wait_ge(S["y_ps"], T)
                nc.scalar.copy(hh[:, k % 2, :], ps_h[:]).then_inc(S["hh_done"], 1)

            def sigmoid(T, k):
                act.wait_ge(S["gc_done"], T + 1)
                if not known(T):
                    act.wait_ge(S["h_done"], T)
                nc.scalar.activation(sg[:], gc[:], ACT.Sigmoid, scale=ALPHA).then_inc(S["sg_done"], 1)

            def scale_y(T, k):
                act.wait_ge(aslot_in[k], slot_count(T, k))
                act.wait_ge(S["y_ps"], T + 2)
                if not known(T, 2):
                    act.wait_ge(S["added"], 16 * (T - 1))
                nc.scalar.mul(yb[:, k % 2, :], ps_y[k % 2][:],
                              aslot[:, k, 1:2].bitcast(fp32)).then_inc(S["y_done"], 1)

            def split_high(T, k, own):
                with act.If(field(act, own, "some")):
                    first, end = field(act, own, "first"), field(act, own, "end")
                    buf = 1 - field(act, own, "buffer")
                    got = field(act, own, "split") * (48 // HC) + 48
                    start = field(act, own, "start")
                    with act.Fori(first, end) as c:
                        act.wait_ge(S["raw_in"], got)
                        act.wait_ge(S["y_ps"], start + 1)
                        nc.scalar.copy(w[:, bass.ds(buf, 1), 0, bass.ds(c, 1), :].rearrange("p a c d -> p (a c d)"),
                                       raw_w[:, bass.ds(c, 1), :].rearrange("p c d -> p (c d)")).then_inc(S["hi_done"], 1)

            def step(T, k):
                own, offs = word(act, 0, T), word(act, 1, T)
                load_slots(field(act, offs, "slots_3"), (k + 3) % UNROLL, gslot, gslot_in)
                if not known(T):
                    high_h(T - 1, (k - 1) % UNROLL)
                high_x(T + 1, (k + 1) % UNROLL)
                split_high(T, k, own)
                sigmoid(T, k)
                if not known(T):
                    scale_y(T - 1, (k - 1) % UNROLL)
                if not known(T, 3):
                    act.wait_ge(S["added"], 16 * (T - 2))
                load_slots(field(act, offs, "slots_1"), (k + 1) % UNROLL, aslot, aslot_in)

            load_slots(0, 0, gslot, gslot_in)
            load_slots(0, 0, aslot, aslot_in)
            act.wait_ge(S["table_done"], 1)
            final = final_lap(act)
            for T in range(1, 3):
                load_slots(field(act, word(act, 1, TABLE - 3 + T), "slots_1"), T, gslot, gslot_in)
            high_x(0, 0)
            for T in range(UNROLL):
                step(T, T)
            with act.Fori(1, final + 1) as lap:
                for k in range(UNROLL):
                    step(UNROLL * lap + k, k)
            high_h(UNROLL * final + (UNROLL - 1), UNROLL - 1)
            scale_y(UNROLL * final + (UNROLL - 1), UNROLL - 1)

        @block.tensor
        def _(pe):
            T_ = nc.tensor.transpose
            pe.wait_ge(S["pool_c"], 5)
            pe.wait_ge(S["const_in"], 96)
            T_(ps_k[:, 0:P], wq_sb[:], ident[:])
            T_(ps_k[:, P:2 * P], wk_sb[:], ident[:])
            for c in range(HC):
                last = T_(ps_rw[:, c * E:(c + 1) * E], rw_sb[:, c * P:(c + 1) * P], ident[0:E, 0:E])
            last.then_inc(S["wT_ps"], 1)
            pe.wait_ge(S["ctx_in_s"], 16)

            def project(b):
                if b:
                    pe.wait_ge(S["qk_done"], 2 * b)
                for r in range(RT):
                    last = T_(ps_q[:, r * P:(r + 1) * P], ctx_sb[:, b * RT + r, :], ident[:])
                last.then_inc(S["ctxT_ps"], 1)
                pe.wait_ge(S["ctxT_done"], b + 1)
                if b == 0:
                    pe.wait_ge(S["wT_done"], 3)
                nc.tensor.matmul(ps_q[:], wqT[:], ctxT[:], start=True, stop=True).then_inc(S["q_ps"], 1)
                nc.tensor.matmul(ps_k[:], wkT[:], ctxT[:], start=True, stop=True).then_inc(S["k_ps"], 1)

            def scores(b):
                pe.wait_ge(S["qk_done"], 2 * b + 2)
                for r in range(RT):
                    i = RT * b + r
                    if i >= 2:
                        pe.wait_ge(S["s_done"], i - 1)
                    nc.tensor.matmul(ps_s[i % 2][:], qT[:, r * P:(r + 1) * P], kT[:], start=True, stop=True).then_inc(S["s_ps"], 1)

            for b in range(2):
                project(b)
                scores(b)
            for b in range(NB):
                pe.wait_ge(S["ok_done"], b + 1)
                if b:
                    pe.wait_ge(S["payload_done"], b)
                nc.tensor.matmul(ps_ok, ones[:], okv[:], start=True, stop=True).then_inc(S["ok_ps"], 1)
                pe.wait_ge(S["a_done"], RT * (b + 1))
                if b:
                    pe.wait_ge(S["scT_done"], b)
                if b:
                    pe.wait_ge(S["bo_done"], RT * b)
                for r in range(RT):
                    i = RT * b + r
                    if i >= 2:
                        pe.wait_ge(S["x1_done"], i - 1)
                    for j in range(RT):
                        last = T_(ps_t[r % 2][:, j * P:(j + 1) * P], A[:, j, r * P:(r + 1) * P], ident[:])
                    last.then_inc(S["at_ps"], 1)
                pe.wait_ge(S["x1_done"], RT * (b + 1))
                for r in range(RT):
                    i = RT * b + r
                    pe.wait_ge(S["xn2_done"], i + 1)
                    if i >= 2:
                        pe.wait_ge(S["xt_done"], i - 1)
                    for c in range(HC):
                        last = T_(ps_t[r % 2][:, c * P:(c + 1) * P], xn2[:, r, c * P:(c + 1) * P], ident[:])
                    last.then_inc(S["xt_ps"], 1)
                if b:
                    pe.wait_ge(S["payload_done"], b)
                pe.wait_ge(S["xt_done"], RT * (b + 1))
                for r in range(RT):
                    for c in range(HC):
                        last = nc.tensor.matmul(ps_logit[:, r * E:(r + 1) * E], xn2T[:, r, c * P:(c + 1) * P],
                                                rwT[:, c * E:(c + 1) * E], start=(c == 0), stop=(c == HC - 1))
                last.then_inc(S["logit_ps"], 1)
                if b + 2 < NB:
                    project(b + 2)
                pe.wait_ge(S["hot_done"], b + 1)
                nc.tensor.matmul(ps_rank, lower[:], onehot[:].rearrange("p r e -> p (r e)"), start=True, stop=False)
                nc.tensor.matmul(ps_rank, ones[:], before[:, b * RT:(b + 1) * RT, :].rearrange("p r e -> p (r e)"),
                                 start=False, stop=True).then_inc(S["rank_ps"], 1)
                if b + 2 < NB:
                    scores(b + 2)
                pe.wait_ge(S["dense_done"], b + 1)
                pe.wait_ge(S["payload_done"], b + 1)
                for r in range(RT):
                    last = T_(ps_scT[:, r * P:(r + 1) * P], dense[:, r, :], ident[:])
                last.then_inc(S["scT_ps"], 1)
                pe.wait_ge(S["scT_done"], b + 1)
                if b == NB - 1:
                    nc.tensor.matmul(ps_rank[:, 0:E], ones[:], before[:, NT, :], start=True, stop=True).then_inc(S["cnt_ps"], 1)
                for r in range(RT):
                    i = RT * b + r
                    if i >= 2:
                        pe.wait_ge(S["bo_done"], i - 1)
                    nc.tensor.matmul(ps_bd[r % 2], denseT[:, r * P:(r + 1) * P], bd_sb[:], start=True, stop=True).then_inc(S["bd_ps"], 1)
            pe.sem_inc(S["y_ps"], 1)
            pe.wait_ge(S["bo_done"], NT)

            def tr_x(T, k):
                pe.wait_ge(gathered[k], slot_count(T, k))
                if not known(T):
                    pe.wait_ge(S["xl_done"], T)
                for c in range(HC):
                    last = T_(ps_x[:, c * P:(c + 1) * P], xg[:, k, c * P:(c + 1) * P], ident[:])
                last.then_inc(S["xT_ps"], 1)

            def tr_h(T, k):
                pe.wait_ge(S["h_done"], T + 1)
                if not known(T):
                    pe.wait_ge(S["hl_done"], T)
                for c in range(HC):
                    last = T_(ps_h[:, c * P:(c + 1) * P], hb[:, k % 2, c * P:(c + 1) * P], ident[:])
                last.then_inc(S["hT_ps"], 1)

            def product(out_ps, high, low, buf, cols):
                n_mm = 3 * HC
                m = 0
                for c in range(HC):
                    rows = slice(c * P, (c + 1) * P)
                    for lhs, part in ((high, 0), (high, 1), (low, 0)):
                        last = nc.tensor.matmul(out_ps, lhs[:, rows],
                                                w[:, bass.ds(buf, 1), part, c, cols].rearrange("p a d -> p (a d)"),
                                                start=(m == 0), stop=(m == n_mm - 1))
                        m += 1
                return last

            def gate_up(T, k, half, buf):
                cols = slice(half * 512, (half + 1) * 512)
                last = product(psG[k % 2][:, cols], xh[:, k % 2, :], xl[:, k % 2, :], buf, cols)
                if half:
                    last.then_inc(S["gu_ps"], 1)

            def down(T, k, buf):
                pe.wait_ge(S["hl_done"], T + 1)
                if not known(T, 2):
                    pe.wait_ge(S["y_done"], T - 1)
                product(ps_y[k % 2][:], hh[:, k % 2, :], hl[:, k % 2, :], buf, slice(GU, WIDE)).then_inc(S["y_ps"], 1)

            def step(T, k):
                own = word(pe, 0, T)
                buf, need = field(pe, own, "buffer"), field(pe, own, "split")
                pe.wait_ge(S["lo_done"], need)
                pe.wait_ge(S["xl_done"], T + 1)
                if not known(T, 2):
                    pe.wait_ge(S["gu_read"], T - 1)
                gate_up(T, k, 0, buf)
                if not known(T):
                    tr_h(T - 1, (k - 1) % UNROLL)
                tr_x(T + 1, (k + 1) % UNROLL)
                gate_up(T, k, 1, buf)
                if not known(T):
                    down(T - 1, (k - 1) % UNROLL, field(pe, own, "buffer_before"))

            tr_x(0, 0)
            pe.wait_ge(S["table_done"], 1)
            final = final_lap(pe)
            for T in range(UNROLL):
                step(T, T)
            with pe.Fori(1, final + 1) as lap:
                for k in range(UNROLL):
                    step(UNROLL * lap + k, k)
            last_tile = UNROLL * final + (UNROLL - 1)
            buf = field(pe, word(pe, 0, last_tile), "buffer")
            tr_h(last_tile, UNROLL - 1)
            down(last_tile, UNROLL - 1, buf)

        @block.vector
        def _(dve):
            n = [0]
            V = nc.vector

            def link(ins):
                n[0] += 1
                ins.then_inc(S["chain"], 1)
                dve.wait_ge(S["chain"], n[0])

            def send(ins):
                n[0] += 1
                ins.then_inc(S["chain"], 1)

            def join():
                dve.wait_ge(S["chain"], n[0])

            dve.wait_ge(S["pool_c"], 15)
            link(V.memset(pad_rows, 0))
            link(V.memset(minus_big[:], -BIG))
            V.memset(zero_rows, 0.0).then_inc(S["dve_c"], 1)
            V.memset(eps_c[:], EPS).then_inc(S["dve_c"], 1)
            V.tensor_scalar(pad_rows[:, :, 0], pad_i, P - 1, TOKENS, ALU.bitwise_and, ALU.bitwise_or).then_inc(S["dve_c"], 1)
            V.memset(before[:, 0, :], 0.0).then_inc(S["dve_c"], 1)
            V.tensor_copy(payload[:, :, 0].rearrange("p (i k) -> p i k", k=TOP_K),
                          token_id[:].bitcast(u32).unsqueeze(2).broadcast_to([P, NT, TOP_K])).then_inc(S["dve_c"], 1)
            dve.wait_ge(S["wT_ps"], 1)
            V.tensor_copy(wqT[:], ps_k[:, 0:P]).then_inc(S["wT_done"], 1)
            V.tensor_copy(wkT[:], ps_k[:, P:2 * P]).then_inc(S["wT_done"], 1)
            V.tensor_copy(rwT[:], ps_rw).then_inc(S["wT_done"], 1)
            dve.wait_ge(S["gam_done"], 1)
            link(V.tensor_scalar(gam[:, 2:3], gam[:, 1:2], 0.5, None, ALU.mult))
            link(V.tensor_scalar(gam[:, 3:4], gam[:, 1:2], -1.0, 1.0, ALU.mult, ALU.add))

            def prepare(b):
                dve.wait_ge(x_in[b], 16)
                for r in range(RT):
                    send(V.bn_stats(st1[:, 1, r, :], x_sb[:, b * RT + r, :]))
                for r in range(RT):
                    dve.wait_ge(S["s_done"], RT * b + r + 1)
                    send(V.bn_stats(st1[:, 0, r, :], sim[:, b % 2, r, :]))
                join()
                for w in range(2):
                    for r in range(RT):
                        ins = V.bn_aggr(mv1[:, w, r, :], st1[:, w, r, :])
                        if w == 0 or r < RT - 1:
                            send(ins)
                join()
                ins.then_inc(S["var1"], 1)
                dve.wait_ge(S["sd1"], b + 1)
                send(V.tensor_scalar(slope[:, b % 2, :], sd1[:, 0, :], 1.0 / (N * DENSITY), None, ALU.mult))
                V.scalar_tensor_tensor(out=nguess[:, b % 2, :], in0=sd1[:, 0, :], scalar=-QUANTILE, in1=mv1[:, 0, :, 0],
                                       op0=ALU.mult, op1=ALU.subtract).then_inc(S["guess_done"], 1)
                link(V.reciprocal(rs[:], sd1[:, 1, :]))
                link(V.tensor_scalar(rs[:], rs[:], gam[:, 3:4], None, ALU.mult))
                link(V.scalar_tensor_tensor(out=b1[:, b % 2, :], in0=mv1[:, 1, :, 0], scalar=-1.0, in1=rs[:],
                                            op0=ALU.mult, op1=ALU.mult))
                V.tensor_scalar(s1[:, b % 2, :], rs[:], 1.0, None, ALU.add).then_inc(S["aff1"], 1)

            def thresholds(b):
                dve.wait_ge(S["moved"], 2 * len(GAINS) * (b + 1))
                link(V.tensor_scalar(guess[:], nguess[:, b % 2, :], -1.0, None, ALU.mult))
                for r in range(RT):
                    link(V.scalar_tensor_tensor(out=marks[:], in0=sim[:, b % 2, r, :], scalar=guess[:, r:r + 1],
                                                in1=minus_big[:].broadcast_to([P, N]), op0=ALU.is_ge, op1=ALU.mult,
                                                accum_out=above[:, r:r + 1]))
                    link(V.tensor_tensor(work[:], marks[:], sim[:, b % 2, r, :], ALU.add))
                    link(V.max(top8[:, r, :], work[:]))
                link(V.tensor_scalar(above[:], above[:], 1.0 / BIG, float(KEEP - 1), ALU.mult, ALU.add))
                link(V.tensor_tensor(pick[:], iota8[:].unsqueeze(1).broadcast_to([P, RT, 8]),
                                     above[:].unsqueeze(2).broadcast_to([P, RT, 8]), ALU.is_equal))
                V.tensor_reduce(okv[:], pick[:], AX.X, ALU.add).then_inc(S["ok_done"], 1)
                dve.wait_ge(S["ok_done"], b + 1)
                link(V.tensor_tensor(pick[:], pick[:], top8[:], ALU.mult))
                link(V.tensor_reduce(thr[:], pick[:], AX.X, ALU.add))
                dve.wait_ge(S["ok_ps"], b + 1)
                link(V.tensor_reduce(okf[:], ps_ok, AX.X, ALU.add))
                link(V.tensor_scalar(oki[:], okf[:], float(P * RT), None, ALU.is_lt))
                failed = dve.value_load(oki[0:1, 0:1], min_val=0, max_val=1)
                with dve.If(failed):
                    for r in range(RT):
                        V.tensor_copy(work[:], sim[:, b % 2, r, :])
                        dve.drain()
                        with dve.Fori(0, (KEEP - 1) // 8):
                            V.max(top8[:, r, :], work[:])
                            dve.drain()
                            V.match_replace(work[:], top8[:, r, :], work[:], NEG)
                            dve.drain()
                        V.max(top8[:, r, :], work[:])
                        dve.drain()
                        V.tensor_copy(thr[:, r:r + 1], top8[:, r, (KEEP - 1) % 8:(KEEP - 1) % 8 + 1])
                        dve.drain()

            def add_bias(b, r):
                dve.wait_ge(S["bd_ps"], RT * b + r + 1)
                V.tensor_tensor(base_out[:, r, :], ps_bd[r % 2], x1[:, r, :], ALU.add).then_inc(S["bo_done"], 1)

            prepare(0)
            dve.wait_ge(S["ctxT_ps"], 2)
            V.tensor_copy(ctxT[:], ps_q[:]).then_inc(S["ctxT_done"], 1)
            dve.wait_ge(S["q_ps"], 2)
            V.tensor_copy(qT[:], ps_q[:]).then_inc(S["qk_done"], 1)
            dve.wait_ge(S["k_ps"], 2)
            V.tensor_copy(kT[:], ps_k[:]).then_inc(S["qk_done"], 1)
            for r in range(RT):
                dve.wait_ge(S["s_ps"], RT + r + 1)
                V.tensor_copy(sim[:, 1, r, :], ps_s[r % 2][:]).then_inc(S["s_done"], 1)
            for b in range(NB):
                if b + 1 < NB:
                    prepare(b + 1)
                thresholds(b)
                dve.wait_ge(S["sig_done"], RT * (b + 1))
                for r in range(RT):
                    V.scalar_tensor_tensor(out=A[:, r, :], in0=sim[:, b % 2, r, :], scalar=thr[:, r:r + 1],
                                           in1=A[:, r, :], op0=ALU.is_ge, op1=ALU.mult).then_inc(S["a_done"], 1)
                dve.wait_ge(S["a_done"], RT * (b + 1))
                dve.wait_ge(S["base_done"], RT * (b + 1))
                for r in range(RT):
                    send(V.scalar_tensor_tensor(out=x_sb[:, RT * b + r, :], in0=A[:, r, :], scalar=gam[:, 2:3],
                                                in1=x_sb[:, RT * b + r, :], op0=ALU.mult, op1=ALU.add))
                join()
                if b:
                    dve.wait_ge(S["xn2_done"], RT * b)
                    dve.wait_ge(S["acc_out"], 16 * b)
                for r in range(RT):
                    dve.wait_ge(S["at_ps"], RT * b + r + 1)
                    V.scalar_tensor_tensor(out=x1[:, r, :], in0=ps_t[r % 2], scalar=gam[:, 2:3],
                                           in1=x_sb[:, RT * b + r, :], op0=ALU.mult, op1=ALU.add).then_inc(S["x1_done"], 1)
                dve.wait_ge(S["x1_done"], RT * (b + 1))
                for r in range(RT):
                    send(V.bn_stats(st[:, r, :], x1[:, r, :]))
                join()
                for r in range(RT):
                    ins = V.bn_aggr(mv[:, r, :], st[:, r, :])
                    if r < RT - 1:
                        send(ins)
                join()
                ins.then_inc(S["var2"], 1)
                dve.wait_ge(S["sd2"], b + 1)
                link(V.reciprocal(r2[:], sd[:]))
                link(V.tensor_tensor(b2[:], mv[:, :, 0], r2[:], ALU.mult))
                V.tensor_scalar(b2[:], b2[:], -1.0, None, ALU.mult).then_inc(S["aff2"], 1)
                dve.wait_ge(S["logit_ps"], b + 1)
                link(V.tensor_tensor(logit[:], ps_logit.rearrange("p (r e) -> p r e", e=E),
                                     rb_sb[:].unsqueeze(1).broadcast_to([P, RT, E]), ALU.add))
                for r in range(RT):
                    link(V.max(best[:, r, :], logit[:, r, :]))
                    link(V.max_index(best_i[:, r, :], best[:, r, :], logit[:, r, :]))
                V.tensor_tensor(dl[:], best[:, :, 0:TOP_K], best[:, :, 0:1].broadcast_to([P, RT, TOP_K]),
                                ALU.subtract).then_inc(S["dl_done"], 1)
                link(V.tensor_copy(ek[:], best_i[:, :, 0:TOP_K]))
                link(V.tensor_tensor(hot[:].rearrange("p r k e -> p (r k) e"),
                                     iota_e[:].unsqueeze(1).broadcast_to([P, RT * TOP_K, E]),
                                     ek[:].rearrange("p r k -> p (r k)").unsqueeze(2).broadcast_to([P, RT * TOP_K, E]),
                                     ALU.is_equal))
                link(V.tensor_reduce(onehot[:], hot[:].rearrange("p r k e -> p r e k"), AX.X, ALU.add))
                for r in range(RT):
                    i = RT * b + r
                    ins = V.tensor_tensor(before[:, i + 1, :], before[:, i, :], onehot[:, r, :], ALU.add)
                    if r < RT - 1:
                        link(ins)
                ins.then_inc(S["hot_done"], 1)
                dve.wait_ge(S["ex_done"], b + 1)
                link(V.tensor_reduce(den[:], ex[:], AX.X, ALU.add))
                link(V.reciprocal(den[:], den[:]))
                link(V.tensor_tensor(score[:], ex[:], den[:].unsqueeze(2).broadcast_to([P, RT, TOP_K]), ALU.mult))
                link(V.tensor_tensor(hotv[:].rearrange("p r k e -> p (r k) e"), hot[:].rearrange("p r k e -> p (r k) e"),
                                     score[:].rearrange("p r k -> p (r k)").unsqueeze(2).broadcast_to([P, RT * TOP_K, E]),
                                     ALU.mult))
                V.tensor_reduce(dense[:], hotv[:].rearrange("p r k e -> p r e k"), AX.X, ALU.add).then_inc(S["dense_done"], 1)
                dve.wait_ge(S["dense_done"], b + 1)
                dve.wait_ge(S["rank_ps"], b + 1)
                link(V.tensor_tensor(pos[:], ps_rank.rearrange("p (r e) -> p r e", e=E),
                                     slot0_e[:].unsqueeze(1).broadcast_to([P, RT, E]), ALU.add))
                for r in range(RT):
                    link(V.tensor_tensor(hotv[:, r], hot[:, r], pos[:, r, :].unsqueeze(1).broadcast_to([P, TOP_K, E]), ALU.mult))
                link(V.tensor_reduce(posk[:], hotv[:], AX.X, ALU.add))
                sl = slice(b * RT * TOP_K, (b + 1) * RT * TOP_K)
                link(V.tensor_copy(slot_i[:, sl], posk[:].rearrange("p r k -> p (r k)")))
                V.tensor_copy(payload[:, sl, 1].bitcast(fp32), score[:].rearrange("p r k -> p (r k)")).then_inc(S["payload_done"], 1)
                dve.wait_ge(S["xn2_done"], RT * (b + 1))
                if b < NB - 1:
                    for r in range(RT):
                        add_bias(b, r)

            dve.wait_ge(S["cnt_ps"], 1)
            link(V.tensor_copy(cnt[:], ps_rank[0:1, 0:E]))
            link(V.tensor_tensor(ncmp, cnt[:].unsqueeze(2).broadcast_to([1, E, E]),
                                 jtab[:].unsqueeze(1).broadcast_to([1, E, E]), ALU.is_gt))
            link(V.tensor_reduce(til[:], ncmp, AX.X, ALU.add))
            link(V.tensor_scalar(til[:], til[:], 1.0, None, ALU.max))
            link(V.tensor_copy(cum[:, 0, :], til[:]))
            src = 0
            for s in (1, 2, 4, 8):
                link(V.tensor_tensor(cum[:, 1 - src, s:E], cum[:, src, s:E], cum[:, src, 0:E - s], ALU.add))
                link(V.tensor_copy(cum[:, 1 - src, 0:s], cum[:, src, 0:s]))
                src = 1 - src
            add_bias(NB - 1, 0)
            add_bias(NB - 1, 1)
            link(V.tensor_scalar(lapj[:], lapj[:], cum[:, src, E - 1:E], None, ALU.is_lt))
            link(V.tensor_reduce(tf[:, 0, 0:1], lapj[:], AX.X, ALU.add))
            link(V.tensor_scalar(laps_tab[:], tf[:, 0, 0:1], -1.0, None, ALU.add))
            link(V.tensor_tensor(cmp_t, ttab[:].unsqueeze(2).broadcast_to([1, TABLE, E]),
                                 cum[:, src, :].unsqueeze(1).broadcast_to([1, TABLE, E]), ALU.is_ge))
            link(V.tensor_reduce(tf[:, 0, :], cmp_t, AX.X, ALU.add))
            link(V.tensor_tensor(cmp_w, cmp_t, til[:].unsqueeze(1).broadcast_to([1, TABLE, E]), ALU.mult))
            link(V.tensor_reduce(tf[:, 1, :], cmp_w, AX.X, ALU.add))
            link(V.tensor_tensor(cmp_w, cmp_t, alt[:].unsqueeze(1).broadcast_to([1, TABLE, E]), ALU.mult))
            link(V.tensor_reduce(tf[:, 2, :], cmp_w, AX.X, ALU.add))
            add_bias(NB - 1, 2)
            add_bias(NB - 1, 3)
            link(V.tensor_tensor(tf[:, 3, :], ttab[:], tf[:, 1, :], ALU.subtract))
            link(V.tensor_scalar(tf[:, 3, :], tf[:, 3, :], float(P), None, ALU.mult))
            link(V.scalar_tensor_tensor(out=tf[:, 3, :], in0=tf[:, 0, :], scalar=float(TOKENS), in1=tf[:, 3, :],
                                        op0=ALU.mult, op1=ALU.add))
            link(V.tensor_scalar(tf[:, 3, :], tf[:, 3, :], float(SLOTS), None, ALU.min))
            tabs = lambda row: tf[:, row, 0:TABLE - 1]
            link(V.tensor_tensor(tabs(4), tf[:, 0, 1:TABLE], tabs(0), ALU.subtract))
            link(V.tensor_scalar(tabs(4), tabs(4), float(HC), None, ALU.mult))
            link(V.tensor_tensor(tabs(5), ttab[:, 0:TABLE - 1], tabs(1), ALU.subtract))
            link(V.tensor_scalar(tabs(5), tabs(5), float(AT_ONCE), None, ALU.mult))
            link(V.tensor_scalar(tabs(6), tabs(5), float(HC), None, ALU.min))
            link(V.tensor_scalar(tabs(5), tabs(5), -float(AT_ONCE), 0.0, ALU.add, ALU.max))
            link(V.tensor_tensor(tabs(6), tabs(6), tabs(4), ALU.max))
            link(V.tensor_scalar(tabs(5), tabs(5), float(HC), None, ALU.min))
            link(V.tensor_tensor(tabs(7), tabs(6), tabs(5), ALU.is_gt))
            link(V.tensor_scalar(tabs(4), tabs(0), float(E - 1), None, ALU.is_lt))
            link(V.tensor_tensor(tabs(7), tabs(7), tabs(4), ALU.mult))
            link(V.scalar_tensor_tensor(out=more_f[:, 0:TABLE - 1], in0=tabs(5), scalar=1.0, in1=tabs(6),
                                        op0=ALU.add, op1=ALU.is_lt))
            link(V.tensor_tensor(more_f[:, 0:TABLE - 1], more_f[:, 0:TABLE - 1], tabs(4), ALU.mult))
            link(V.tensor_scalar(tabs(5), tabs(5), float(HC - 1), None, ALU.min))
            link(V.tensor_scalar(tabs(0), tabs(0), float(E - 1), None, ALU.min))
            link(V.tensor_scalar(tabs(0), tabs(0), 1.0, float(HC), ALU.add, ALU.mult))
            link(V.tensor_scalar(tabs(1), tabs(1), float(TILES), None, ALU.min))
            link(V.memset(word_f, 0.0))
            for value, name in ((tabs(2), "buffer"), (tabs(7), "some"), (more_f[:, 0:TABLE - 1], "more"),
                                (tabs(5), "first"), (tabs(6), "end"), (tabs(0), "split"), (tabs(1), "start")):
                link(V.scalar_tensor_tensor(out=word_f[:, 0, 0:TABLE - 1], in0=value, scalar=float(1 << FIELDS[name][0]),
                                            in1=word_f[:, 0, 0:TABLE - 1], op0=ALU.mult, op1=ALU.add))
            link(V.scalar_tensor_tensor(out=word_f[:, 0, 1:TABLE], in0=tf[:, 2, 0:TABLE - 1],
                                        scalar=float(1 << FIELDS["buffer_before"][0]),
                                        in1=word_f[:, 0, 1:TABLE], op0=ALU.mult, op1=ALU.add))
            link(V.tensor_scalar(tabs(3), tabs(3), 1.0 / P, None, ALU.mult))
            link(V.scalar_tensor_tensor(out=word_f[:, 1, 0:TABLE - 4], in0=tf[:, 3, 3:TABLE - 1],
                                        scalar=float(1 << FIELDS["slots_3"][0]), in1=tf[:, 3, 1:TABLE - 3],
                                        op0=ALU.mult, op1=ALU.add))
            link(V.tensor_copy(word_f[:, 1, TABLE - 3:TABLE], tf[:, 3, 0:3]))
            V.tensor_copy(tile_tab[:], word_f).then_inc(S["table_done"], 1)
            dve.wait_ge(S["table_done"], 1)
            dve.wait_ge(S["slots_done"], 1)
            dve.wait_ge(S["acc_out"], 16 * NB)
            dve.wait_ge(S["xn2_out"], 16 * NB)

            c0 = n[0]

            def low_x(T, k):
                dve.wait_ge(S["xh_done"], T + 1)
                V.tensor_tensor(xl[:, k % 2, :], ps_x[:], xh[:, k % 2, :].bitcast(fp32),
                                ALU.subtract).then_inc(S["xl_done"], 1)

            def low_h(T, k):
                dve.wait_ge(S["hh_done"], T + 1)
                V.tensor_tensor(hl[:, k % 2, :], ps_h[:], hh[:, k % 2, :].bitcast(fp32),
                                ALU.subtract).then_inc(S["hl_done"], 1)

            def gate(T, k, buf):
                dve.wait_ge(S["gu_ps"], T + 1)
                V.tensor_tensor(gu[:], psG[k % 2][:], bgu[:, bass.ds(buf, 1), :].rearrange("p a d -> p (a d)"),
                                ALU.add).then_inc(S["gu_read"], 1)
                dve.wait_ge(S["gu_read"], T + 1)
                gv = gu[:].rearrange("p (d t) -> p t d", t=2)
                V.tensor_scalar(gc[:], gv[:, 0, :], LIMIT, None, ALU.min).then_inc(S["gc_done"], 1)
                V.tensor_scalar(uc[:], gv[:, 1, :], LIMIT, -LIMIT, ALU.min, ALU.max).then_inc(S["chain"], 1)
                dve.wait_ge(S["chain"], 2 * T + (c0 + 1))
                dve.wait_ge(S["gc_done"], T + 1)
                V.scalar_tensor_tensor(out=h1[:], in0=uc[:], scalar=1.0, in1=gc[:], op0=ALU.add,
                                       op1=ALU.mult).then_inc(S["chain"], 1)
                dve.wait_ge(S["chain"], 2 * T + (c0 + 2))
                dve.wait_ge(S["sg_done"], T + 1)
                if not known(T, 2):
                    dve.wait_ge(S["hT_ps"], T - 1)
                V.tensor_tensor(hb[:, k % 2, :], h1[:], sg[:], ALU.mult).then_inc(S["h_done"], 1)

            def split_chunk(c, nbuf, need):
                dve.wait_ge(S["hi_done"], need + c + 1)
                bcols = bgu[:].rearrange("p a (c d) -> p a c d", c=HC)
                V.tensor_copy(bcols[:, bass.ds(nbuf, 1), bass.ds(c, 1), :].rearrange("p a c d -> p (a c d)"),
                              raw_b[:, bass.ds(c, 1), :].rearrange("p c d -> p (c d)"))
                V.tensor_tensor(w[:, bass.ds(nbuf, 1), 1, bass.ds(c, 1), :].rearrange("p a c d -> p (a c d)"),
                                raw_w[:, bass.ds(c, 1), :].rearrange("p c d -> p (c d)"),
                                w[:, bass.ds(nbuf, 1), 0, bass.ds(c, 1), :].rearrange("p a c d -> p (a c d)").bitcast(fp32),
                                ALU.subtract).then_inc(S["lo_done"], 1)

            def step(T, k):
                own = word(dve, 0, T)
                buf = field(dve, own, "buffer")
                if not known(T):
                    low_h(T - 1, (k - 1) % UNROLL)
                low_x(T + 1, (k + 1) % UNROLL)
                with dve.If(field(dve, own, "some")):
                    split_chunk(field(dve, own, "first"), 1 - buf, field(dve, own, "split"))
                gate(T, k, buf)
                with dve.If(field(dve, own, "more")):
                    nbuf, split = dve.snap(1 - buf, min_val=0, max_val=1), field(dve, own, "split")
                    with dve.Fori(field(dve, own, "first") + 1, field(dve, own, "end")) as c:
                        split_chunk(c, nbuf, split)

            final = final_lap(dve)
            low_x(0, 0)
            for T in range(UNROLL):
                step(T, T)
            with dve.Fori(1, final + 1) as lap:
                for k in range(UNROLL):
                    step(UNROLL * lap + k, k)
            low_h(UNROLL * final + (UNROLL - 1), UNROLL - 1)


_INS = ["x", "ctx_512", "L0_xattn_Wq", "L0_xattn_Wk", "L0_xattn_gamma_raw", "L0_ffn_router_weight",
        "L0_ffn_router_bias", "L0_ffn_gate_up_proj", "L0_ffn_gate_up_proj_bias", "L0_ffn_down_proj",
        "L0_ffn_down_proj_bias"]
_OUTS = [((4, 512, 512), "float32")]


def kernel(**inputs):
    import numpy as _np
    import concourse.bacc as _bacc
    from concourse import mybir as _mybir
    from concourse.bass_utils import run_bass_kernel_spmd as _run

    nc = _bacc.Bacc("TRN2", target_bir_lowering=False, num_devices=1)
    arrays, args = {}, []
    for name in _INS:
        a = _np.ascontiguousarray(_np.atleast_1d(_np.asarray(inputs[name])))
        arrays[f"in_{name}_dram"] = a
        args.append(nc.dram_tensor(f"in_{name}_dram", a.shape, _mybir.dt.from_np(a.dtype), kind="ExternalInput").ap())
    for i, (shape, dtype) in enumerate(_OUTS):
        dt = _mybir.dt.from_np(_np.dtype(dtype))
        args.append(nc.dram_tensor(f"out_{i}_dram", shape, dt, kind="ExternalOutput").ap())
    xattn_moe_kernel(nc, *args)
    r = _run(nc, [arrays], core_ids=[0])
    return r.results[0]["out_0_dram"]
```

```python
import concourse.bass as bass
from concourse import mybir
from contextlib import ExitStack

P = 128
NB, N, H = 4, 512, 512
C = 128
HEADS = 4
E, TOP_K, D = 16, 4, 512
RT = N // P
NT = NB * RT
TOKENS = NB * N
HC = H // P
KEEP = max(1, int(N * 0.3))
SIM_SCALE = 1.0 / ((C // HEADS) ** 0.5 * HEADS)
ALPHA, LIMIT = 1.702, 7.0
EPS = 1e-5
NEG = -3.0e38
GAINS = (0.8, 0.7, 0.6, 0.5, 0.4, 0.3)
QUANTILE, DENSITY = 0.54, 0.345
AIM = KEEP - 4.5
BIG = 2.0 ** 100
UNROLL = 4
TILES = -(-(TOKENS * TOP_K // P + E - 1) // UNROLL) * UNROLL
SLOTS = E * TOKENS
GU = 2 * D
WIDE = GU + H
TABLE = TILES + 4
LAPS = TILES // UNROLL
FIELDS = {"expert": (0, 4, E - 1), "buffer": (0, 1, 1), "early_0": (4, 1, 1), "early_1": (5, 1, 1),
          "late_0": (6, 1, 1), "late_1": (7, 1, 1), "start": (8, 7, TILES), "bias": (15, 2, 2),
          "buffer_before": (17, 1, 1),
          "slots_1": (0, 9, SLOTS // P), "slots_3": (9, 9, SLOTS // P)}
HALF = HC // 2


def xattn_moe_kernel(nc, x, ctx_in, wq, wk, gamma_raw, rw, rb, gup, gupb, dwn, dwnb, out):
    f32r = mybir.dt.float32r
    fp32, u32, i32 = mybir.dt.float32, mybir.dt.uint32, mybir.dt.int32
    ALU = mybir.AluOpType
    ACT = mybir.ActivationFunctionType
    AX = mybir.AxisListType

    x_v = x.rearrange("b (r p) h -> p (b r) h", p=P)
    ctx_v = ctx_in.rearrange("b (r p) c -> p (b r) c", p=P)
    out_v = out.rearrange("b n h -> (b n) h")
    gup_v = gup.rearrange("e (c p) d -> e p c d", p=P)
    dwn_v = dwn.rearrange("e (c p) h -> e p c h", p=P)

    xn_d = nc.dram_tensor("xn_rows", [TOKENS + P, H], fp32, kind="Internal").ap()
    acc_d = nc.dram_tensor("acc_rows", [TOKENS + P, H], fp32, kind="Internal").ap()
    slot_d = nc.dram_tensor("slot_rows", [SLOTS + P, 2], u32, kind="Internal").ap()

    ctx = ExitStack()
    with ctx:
        def sb(name, shape, dt=fp32):
            return ctx.enter_context(nc.sbuf_tensor(name, shape, dt))

        def sem(name):
            return ctx.enter_context(nc.semaphore(name))

        banks = [ctx.enter_context(nc.psum_tensor(f"bank{i}", [P, 512], fp32)) for i in range(2)]
        bank67 = [ctx.enter_context(nc.psum_tensor(f"bank{i}", [P, 512], fp32)) for i in range(2, 4)]
        psG = [ctx.enter_context(nc.psum_tensor(f"gate_up_ps{i}", [P, GU], fp32)) for i in range(2)]
        ps_q, ps_k = banks
        ps_s = bank67
        ps_t = [psG[0][:, 0:512], psG[0][:, 512:1024]]
        ps_bd = [psG[1][:, 0:512], psG[0][:, 512:1024]]
        ps_m = psG[1][:, 512:1024]
        ps_logit = ps_m[:, 0:RT * E]
        ps_rank = ps_m[:, 64:64 + RT * E]
        ps_rw = ps_m[:, 128:128 + HC * E]
        ps_ok = ps_bd[0][:, 0:RT]
        ps_scT = ps_t[0][0:E, :]
        ps_x, ps_h = banks
        ps_y = bank67

        raw_w = sb("raw_w", [P, HC, WIDE])
        bgu = sb("bgu", [P, 3, GU])
        gslot = sb("gslot", [P, UNROLL, 2], u32)
        aslot = sb("aslot", [P, UNROLL, 2], u32)
        ident = sb("ident", [P, P])
        tile_tab = sb("tile_tab", [1, 2, TABLE], i32)
        laps_tab = sb("laps_tab", [1, 1], i32)
        slot_i = sb("slot_i", [P, NT * TOP_K], u32)
        payload = sb("payload", [P, NT * TOP_K, 2], u32)
        at = -(-nc.sbuf_base // 64) * 64
        half_bytes = 2 * HC * WIDE * 4
        w = nc.alloc_sbuf_tensor_at("w", [P, 2, 2, HC, WIDE], f32r, offset=at)
        even_half = sb("even_half", [P, half_bytes // 4 + 16])
        free = [at + 2 * half_bytes]

        def tile_sb(name, shape, dt=fp32):
            n = 4
            for d in shape[1:]:
                n *= d
            t = nc.alloc_sbuf_tensor_at(name, shape, dt, offset=free[0])
            free[0] += -(-n // 64) * 64
            return t

        xg = tile_sb("xg", [P, UNROLL, H])
        xh, xl = tile_sb("xh", [P, 2, H], f32r), tile_sb("xl", [P, 2, H], f32r)
        gu = tile_sb("gu", [P, GU])
        gc, uc = tile_sb("gc", [P, D]), tile_sb("uc", [P, D])
        sg, h1 = tile_sb("sg", [P, D]), tile_sb("h1", [P, D])
        hb = tile_sb("hb", [P, 2, D])
        hh, hl = tile_sb("hh", [P, 2, D], f32r), tile_sb("hl", [P, 2, D], f32r)
        yb = tile_sb("yb", [P, 2, H])

        x_sb = sb("x_sb", [P, NT, H])
        ctx_sb = sb("ctx_sb", [P, NT, C])
        wq_sb, wk_sb = sb("wq_sb", [P, C]), sb("wk_sb", [P, C])
        wqT, wkT = sb("wqT", [P, C]), sb("wkT", [P, C])
        rw_sb = sb("rw_sb", [E, H])
        rwT = sb("rwT", [P, HC * E])
        rb_sb = sb("rb_sb", [P, E])
        bd_sb = sb("bd_sb", [E, H])
        lower = sb("lower", [P, P])
        ones = sb("ones", [P, P])
        iota_e = sb("iota_e", [P, E])
        slot0_e = sb("slot0_e", [P, E])
        token_id = sb("token_id", [P, NT], i32)
        gam = sb("gam", [P, 4])
        eps_c = sb("eps_c", [P, 1])
        ctxT, qT, kT = sb("ctxT", [P, N]), sb("qT", [P, N]), sb("kT", [P, N])
        sim = sb("sim", [P, 2, RT, N])
        work = sb("work", [P, 2, N])
        junk = sb("junk", [P, RT, N], mybir.dt.bfloat16)
        minus_big = sb("minus_big", [P, 1])
        iota8 = sb("iota8", [P, 8])
        top8 = sb("top8", [P, RT, 8])
        pick = sb("pick", [P, RT, 8])
        above = sb("above", [P, RT])
        okv = sb("okv", [P, RT])
        okf = sb("okf", [P, 1])
        oki = sb("oki", [P, 1], i32)
        guess = sb("guess", [P, RT])
        nguess = sb("nguess", [P, 2, RT])
        slope = sb("slope", [P, 2, RT])
        signs = sb("signs", [P, 2, RT])
        step_u = sb("step_u", [P, 2, RT])
        st1 = sb("st1", [P, 2, RT, 6])
        mv1 = sb("mv1", [P, 2, RT, 2])
        sd1 = sb("sd1", [P, 2, RT])
        thr = sb("thr", [P, RT])
        A = sb("A", [P, RT, N])
        pads = (SLOTS + P) // P
        pad_i = A[:, 0, 0:pads].bitcast(i32)
        pad_rows = A[:].rearrange("p r n -> p (r n)")[:, N:N + 2 * pads].bitcast(i32).rearrange("p (a t) -> p a t", t=2)
        zero_rows = A[:, 3, :]
        x1 = sb("x1", [P, RT, N])
        xn2 = sb("xn2", [P, RT, N])
        xn2T = sb("xn2T", [P, RT, N])
        st = sb("st", [P, RT, 6])
        mv = sb("mv", [P, RT, 2])
        sd = sb("sd", [P, RT])
        rs = sb("rs", [P, RT])
        s1, b1 = sb("s1", [P, 2, RT]), sb("b1", [P, 2, RT])
        r2, b2 = sb("r2", [P, RT]), sb("b2", [P, RT])
        logit = sb("logit", [P, RT, E])
        best = sb("best", [P, RT, 8])
        best_i = sb("best_i", [P, RT, 8], u32)
        ek = sb("ek", [P, RT, TOP_K])
        dl = sb("dl", [P, RT, TOP_K])
        ex = sb("ex", [P, RT, TOP_K])
        den = sb("den", [P, RT])
        score = sb("score", [P, RT, TOP_K])
        hot = sb("hot", [P, RT, TOP_K, E])
        hotv = sb("hotv", [P, RT, TOP_K, E])
        onehot = sb("onehot", [P, RT, E])
        before = sb("before", [P, NT + 1, E])
        dense = sb("dense", [P, RT, E])
        denseT = sb("denseT", [E, RT * P])
        pos = sb("pos", [P, RT, E])
        posk = sb("posk", [P, RT, TOP_K])
        base_out = x1
        cnt = sb("cnt", [1, E])
        jtab = sb("jtab", [1, E])
        til = sb("til", [1, E])
        cum = sb("cum", [1, 2, E])
        ttab = sb("ttab", [1, TABLE])
        flat_a, flat_x = A[0:1].rearrange("p r n -> p (r n)"), xn2T[0:1].rearrange("p r n -> p (r n)")
        cmp_t = flat_a[:, 0:TABLE * E].rearrange("p (t e) -> p t e", e=E)
        tf = flat_a[:, TABLE * E:TABLE * (E + 8)].rearrange("p (w t) -> p w t", w=8)
        cmp_w = flat_x[:, 0:TABLE * E].rearrange("p (t e) -> p t e", e=E)
        word_f = flat_x[:, TABLE * (E + 1) + E * E:TABLE * (E + 3) + E * E].rearrange("p (w t) -> p w t", w=2)
        ncmp = flat_x[:, TABLE * E:TABLE * E + E * E].rearrange("p (t e) -> p t e", e=E)
        lapj = sb("lapj", [1, LAPS])
        S = {}
        for name in ("const_in", "ctx_in_s", "ctx_rest_in", "pad_out", "pool_c", "dve_c", "wT_ps", "wT_done", "gam_done",
                     "ctxT_ps", "ctxT_done", "q_ps", "k_ps", "qk_done", "s_ps", "s_done", "sig_done",
                     "a_done", "at_ps", "x1_done", "var1", "sd1", "aff1", "base_done", "var2", "sd2", "aff2",
                     "xn2_done", "xn2_out", "xt_ps", "xt_done", "logit_ps", "dl_done", "ex_done", "hot_done",
                     "rank_ps", "dense_done", "scT_ps", "scT_done", "bd_ps", "bo_done", "acc_out", "slots_done",
                     "payload_done", "scat", "chain", "cnt_ps", "table_done", "guess_done", "counted", "moved", "ok_done", "ok_ps",
                     "raw_in0", "raw_in1", "hi_done", "lo_done", "xT_ps", "xh_done", "xl_done", "gu_ps", "gu_read", "gc_done", "sg_done",
                     "h_done", "hT_ps", "hh_done", "hl_done", "y_ps", "y_done", "added",
                     "fin", "all_added", "achain", "pchain", "turn"):
            S[name] = sem(name)
        x_in = [sem(f"x_in{b}") for b in range(NB)]
        gslot_in = [sem(f"gslot_in{k}") for k in range(UNROLL)]
        aslot_in = [sem(f"aslot_in{k}") for k in range(UNROLL)]
        gathered = [sem(f"gathered{k}") for k in range(UNROLL)]

        def known(T, below=1):
            return isinstance(T, int) and T < below

        def word(eng, row, T):
            cell = tile_tab[0:1, row, T:T + 1] if isinstance(T, int) else tile_tab[0:1, row, bass.ds(T, 1)]
            return eng.value_load(cell, min_val=0, max_val=(1 << 24) - 1)

        def field(eng, value, name):
            at_bit, bits, most = FIELDS[name]
            return nc.s_assert_within(eng.snap((value >> at_bit) & ((1 << bits) - 1)), 0, most,
                                      skip_runtime_bounds_check_because="the table is built within these bounds")

        def final_lap(eng):
            return eng.value_load(laps_tab[0:1, 0:1], min_val=TOKENS * TOP_K // P // UNROLL - 1, max_val=LAPS - 1)

        def slot_count(T, k):
            return 16 * ((T - k) // UNROLL + 1) if isinstance(T, int) else 4 * (T - k) + 16

        block = ctx.enter_context(nc.Block())

        @block.sync
        def _(sp):
            sp.dma_start(wq_sb[:], wq).then_inc(S["const_in"], 16)
            sp.dma_start(wk_sb[:], wk).then_inc(S["const_in"], 16)
            sp.dma_start(ctx_sb[:, 0:RT, :], ctx_v[:, 0:RT, :]).then_inc(S["ctx_in_s"], 16)
            sp.dma_start(rw_sb[:], rw).then_inc(S["const_in"], 16)
            sp.dma_start(bd_sb[:], dwnb).then_inc(S["const_in"], 16)
            sp.dma_start(rb_sb[:], rb.rearrange("(a e) -> a e", a=1).broadcast_to([P, E])).then_inc(S["const_in"], 16)
            sp.dma_start(gam[:, 0:1], gamma_raw.rearrange("(a e) -> a e", a=1).broadcast_to([P, 1])).then_inc(S["const_in"], 16)
            sp.dma_start(ctx_sb[:, RT:NT, :], ctx_v[:, RT:NT, :]).then_inc(S["ctx_rest_in"], 16)
            for b in range(NB):
                sp.dma_start(x_sb[:, b * RT:(b + 1) * RT, :], x_v[:, b * RT:(b + 1) * RT, :]).then_inc(x_in[b], 16)
            sp.wait_ge(S["dve_c"], 3)
            sp.dma_start(slot_d.rearrange("(p a) t -> p a t", p=P), pad_rows.bitcast(u32)).then_inc(S["pad_out"], 16)
            sp.dma_start(xn_d[TOKENS:TOKENS + P, :], zero_rows).then_inc(S["pad_out"], 16)
            sp.dma_start(acc_d[TOKENS:TOKENS + P, :], zero_rows).then_inc(S["pad_out"], 16)

            def load_half(e, h, bias_at):
                chunks = slice(HALF * h, HALF * (h + 1))
                gate_up, down, bias = (gup_v[e], dwn_v[e], gupb[e:e + 1, :]) if isinstance(e, int) else (
                    gup_v[bass.ds(e, 1)].rearrange("a p c d -> p (a c) d"),
                    dwn_v[bass.ds(e, 1)].rearrange("a p c d -> p (a c) d"), gupb[bass.ds(e, 1), :])
                done = S[f"raw_in{h}"]
                sp.dma_start(raw_w[:, chunks, 0:GU], gate_up[:, chunks, :]).then_inc(done, 16)
                sp.dma_start(raw_w[:, chunks, GU:WIDE], down[:, chunks, :]).then_inc(done, 16)
                if h == 0:
                    sp.dma_start(bgu[:, bias_at, :], bias.broadcast_to([P, GU])).then_inc(done, 16)

            load_half(0, 0, 0)
            load_half(0, 1, 0)
            for b in range(NB):
                rows = slice(b * N, (b + 1) * N)
                if b >= 2:
                    sp.wait_ge(S["lo_done"], HALF * (b - 1))
                    load_half(1, b - 2, 1)
                sp.wait_ge(S["xn2_done"], RT * (b + 1))
                sp.dma_start(xn_d[rows, :].rearrange("(r p) h -> p r h", p=P), xn2[:]).then_inc(S["xn2_out"], 16)
                sp.wait_ge(S["bo_done"], RT * (b + 1))
                sp.dma_start(acc_d[rows, :].rearrange("(r p) h -> p r h", p=P), base_out[:]).then_inc(S["acc_out"], 16)
            for e in range(2, min(4, E)):
                for h in range(2):
                    sp.wait_ge(S["lo_done"], HC * (e - 1) + HALF * (h + 1))
                    load_half(e, h, e % 3)
            with sp.Fori(1, (E - 1) // 3) as trio:
                for j in range(1, 4):
                    for h in range(2):
                        sp.wait_ge(S["lo_done"], HC * 3 * trio + (HC * (j - 1) + HALF * (h + 1)))
                        load_half(3 * trio + j, h, j % 3)
            sp.wait_ge(S["all_added"], 1)
            sp.dma_start(out_v, acc_d[0:TOKENS, :]).then_inc(S["fin"], 16)
            sp.wait_ge(S["fin"], 16)

        @block.gpsimd
        def _(pool):
            c = S["pool_c"]
            pool.memset(ident[:], 0.0).then_inc(c, 1)
            pool.memset(lower[:], 1.0).then_inc(c, 1)
            pool.memset(ones[:], 1.0).then_inc(c, 1)
            pool.wait_ge(c, 3)
            pool.affine_select(out=ident[:], in_=ident[:], compare_op=ALU.not_equal, fill=1.0, base=0,
                               pattern=[[-1, P]], channel_multiplier=1).then_inc(c, 1)
            pool.affine_select(out=lower[:], in_=lower[:], compare_op=ALU.is_gt, fill=0.0, base=0,
                               pattern=[[1, P]], channel_multiplier=-1).then_inc(c, 1)
            kw = dict(allow_small_or_imprecise_dtypes=True)
            pool.iota(iota_e[:], pattern=[[1, E]], base=0, channel_multiplier=0, **kw).then_inc(c, 1)
            pool.iota(slot0_e[:], pattern=[[TOKENS, E]], base=0, channel_multiplier=0, **kw).then_inc(c, 1)
            pool.iota(token_id[:], pattern=[[P, NT]], base=0, channel_multiplier=1).then_inc(c, 1)
            pool.iota(pad_i, pattern=[[1, (SLOTS + P) // P]], base=0, channel_multiplier=1).then_inc(c, 1)
            pool.iota(jtab[:], pattern=[[P, E]], base=0, channel_multiplier=0, **kw).then_inc(c, 1)
            pool.iota(ttab[:], pattern=[[1, TABLE]], base=0, channel_multiplier=0, **kw).then_inc(c, 1)
            pool.iota(lapj[:], pattern=[[UNROLL, LAPS]], base=0, channel_multiplier=0, **kw).then_inc(c, 1)
            pool.iota(iota8[:], pattern=[[1, 8]], base=0, channel_multiplier=0, **kw).then_inc(c, 1)
            n = [0]

            def link(ins):
                n[0] += 1
                ins.then_inc(S["pchain"], 1)
                pool.wait_ge(S["pchain"], n[0])

            scattered = [0]

            def scatter(batches, count):
                for k in range(scattered[0], min(scattered[0] + count, batches * RT * TOP_K)):
                    if k == 0:
                        pool.wait_ge(S["pad_out"], 48)
                    if k % (RT * TOP_K) == 0:
                        pool.wait_ge(S["payload_done"], k // (RT * TOP_K) + 1)
                    pool.indirect_dma_start(slot_d, bass.IndirectOffsetOnAxis(slot_i[:, k:k + 1], 0),
                                            payload[:, k, :], None).then_inc(S["scat"], 16)
                    scattered[0] += 1

            for b in range(NB):
                for it, gain in enumerate(GAINS):
                    for h in range(2):
                        rr = slice(2 * h, 2 * h + 2)
                        pool.wait_ge(S["counted"], RT * (len(GAINS) * b + it) + 2 * h + 2)
                        link(pool.tensor_scalar(step_u[:, h, 0:2], signs[:, b % 2, rr], float(N - 2 * AIM),
                                                -gain / 2, ALU.add, ALU.mult))
                        link(pool.tensor_tensor(step_u[:, h, 2:4], step_u[:, h, 0:2], slope[:, b % 2, rr], ALU.mult))
                        pool.tensor_tensor(nguess[:, b % 2, rr], nguess[:, b % 2, rr], step_u[:, h, 2:4],
                                           ALU.add).then_inc(S["moved"], 1)
                        if b >= 2:
                            scatter(b - 1, 1)
                pool.wait_ge(S[f"raw_in{b // HALF}"], 48 if b < HALF else 32)
                pool.tensor_copy(w[:, 0, 0, b, :], raw_w[:, b, :]).then_inc(S["hi_done"], 1)
                pool.wait_ge(S["hi_done"], b + 1)
                pool.tensor_tensor(w[:, 0, 1, b, :], raw_w[:, b, :], w[:, 0, 0, b, :].bitcast(fp32),
                                   ALU.subtract).then_inc(S["lo_done"], 1)
            scatter(NB, NT * TOP_K)
            pool.wait_ge(S["scat"], 16 * NT * TOP_K)
            pool.sem_inc(S["slots_done"], 1)
            pool.wait_ge(S["xn2_out"], 16 * NB)
            pool.wait_ge(S["acc_out"], 16 * NB)

            def gather(T, k):
                pool.wait_ge(gslot_in[k], slot_count(T, k))
                if not known(T, UNROLL):
                    pool.wait_ge(S["xT_ps"], T - UNROLL + 1)
                pool.sem_inc(S["turn"], 1)
                pool.indirect_dma_start(xg[:, k, :], None, xn_d,
                                        bass.IndirectOffsetOnAxis(gslot[:, k, 0:1], 0)).then_inc(gathered[k], 16)

            def add(T, k):
                pool.wait_ge(S["y_done"], T + 1)
                if not known(T):
                    pool.wait_ge(S["added"], 16 * T)
                pool.sem_inc(S["turn"], 1)
                pool.indirect_dma_start(acc_d, bass.IndirectOffsetOnAxis(aslot[:, k, 0:1], 0),
                                        yb[:, k % 2, :], None, compute_op=ALU.add).then_inc(S["added"], 16)

            def step(T, k):
                gather(T + 2, (k + 2) % UNROLL)
                if not known(T):
                    add(T - 1, (k - 1) % UNROLL)

            gather(0, 0)
            pool.wait_ge(S["table_done"], 1)
            final = final_lap(pool)
            gather(1, 1)
            for T in range(UNROLL):
                step(T, T)
            with pool.Fori(1, final + 1) as lap:
                for k in range(UNROLL):
                    step(UNROLL * lap + k, k)
            add(UNROLL * final + (UNROLL - 1), UNROLL - 1)
            pool.wait_ge(S["added"], 16 * UNROLL * final + 16 * UNROLL)
            pool.sem_inc(S["all_added"], 1)
            for k in range(2):
                pool.wait_ge(gathered[k], 16 * final + 32)
            pool.wait_ge(aslot_in[0], 16 * final + 32)
            pool.wait_ge(gslot_in[2], 16 * final + 32)
            pool.sem_inc(S["turn"], 1)

        @block.scalar
        def _(act):
            n = [0]

            def link(ins):
                n[0] += 1
                ins.then_inc(S["achain"], 1)
                act.wait_ge(S["achain"], n[0])

            act.wait_ge(S["const_in"], 96)
            nc.scalar.activation(gam[:, 1:2], gam[:, 0:1], ACT.Sigmoid).then_inc(S["gam_done"], 1)

            def project(b):
                act.wait_ge(S["ctxT_ps"], b + 1)
                if b:
                    act.wait_ge(S["k_ps"], b)
                nc.scalar.copy(ctxT[:], ps_q[:]).then_inc(S["ctxT_done"], 1)
                if b:
                    act.wait_ge(S["s_ps"], RT * b)
                act.wait_ge(S["q_ps"], b + 1)
                nc.scalar.copy(qT[:], ps_q[:]).then_inc(S["qk_done"], 1)
                act.wait_ge(S["k_ps"], b + 1)
                nc.scalar.copy(kT[:], ps_k[:]).then_inc(S["qk_done"], 1)

            def scores(b):
                for r in range(RT):
                    i = RT * b + r
                    act.wait_ge(S["s_ps"], i + 1)
                    if b >= 2:
                        act.wait_ge(S["a_done"], RT * (b - 1))
                    nc.scalar.copy(sim[:, b % 2, r, :], ps_s[i % 2][:]).then_inc(S["s_done"], 1)

            def deviations(b):
                act.wait_ge(S["var1"], b + 1)
                nc.scalar.activation(sd1[:], mv1[:, :, :, 1], ACT.Sqrt, bias=eps_c[:]).then_inc(S["sd1"], 1)

            def search(b):
                act.wait_ge(S["guess_done"], b + 1)
                if b:
                    act.wait_ge(S["counted"], RT * len(GAINS) * b)
                for it in range(len(GAINS)):
                    for r in range(RT):
                        if it and r % 2 == 0:
                            act.wait_ge(S["moved"], 2 * (len(GAINS) * b + it - 1) + r // 2 + 1)
                        nc.scalar.activation(junk[:, r, :], sim[:, b % 2, r, :], ACT.Sign, bias=nguess[:, b % 2, r:r + 1],
                                             accum_out=signs[:, b % 2, r:r + 1]).then_inc(S["counted"], 1)

            def gates(b):
                if b:
                    act.wait_ge(S["x1_done"], RT * b)
                    act.wait_ge(S["at_ps"], RT * b)
                else:
                    act.wait_ge(S["pad_out"], 48)
                for r in range(RT):
                    nc.scalar.activation(A[:, r, :], sim[:, b % 2, r, :], ACT.Sigmoid, scale=SIM_SCALE).then_inc(S["sig_done"], 1)
                act.wait_ge(S["aff1"], b + 1)
                for r in range(RT):
                    nc.scalar.activation(x_sb[:, RT * b + r, :], x_sb[:, RT * b + r, :], ACT.Identity,
                                         bias=b1[:, b % 2, r:r + 1], scale=s1[:, b % 2, r:r + 1]).then_inc(S["base_done"], 1)

            def norm(b):
                act.wait_ge(S["var2"], b + 1)
                nc.scalar.activation(sd[:], mv[:, :, 1], ACT.Sqrt, bias=eps_c[:]).then_inc(S["sd2"], 1)
                act.wait_ge(S["aff2"], b + 1)
                if b:
                    act.wait_ge(S["xn2_out"], 16 * b)
                    act.wait_ge(S["xt_ps"], RT * b)
                for r in range(RT):
                    nc.scalar.activation(xn2[:, r, :], x1[:, r, :], ACT.Identity,
                                         bias=b2[:, r:r + 1], scale=r2[:, r:r + 1]).then_inc(S["xn2_done"], 1)
                if b:
                    act.wait_ge(S["logit_ps"], b)
                for r in range(RT):
                    act.wait_ge(S["xt_ps"], RT * b + r + 1)
                    nc.scalar.copy(xn2T[:, r, :], ps_t[r % 2]).then_inc(S["xt_done"], 1)

            def exponentials(b):
                act.wait_ge(S["dl_done"], b + 1)
                nc.scalar.activation(ex[:], dl[:], ACT.Exp).then_inc(S["ex_done"], 1)

            def routed(b):
                act.wait_ge(S["scT_ps"], b + 1)
                if b:
                    act.wait_ge(S["bd_ps"], RT * b)
                nc.scalar.copy(denseT[:], ps_scT).then_inc(S["scT_done"], 1)

            project(0)
            scores(0)
            deviations(0)
            search(0)
            deviations(1)
            gates(0)
            for b in range(NB):
                if b + 1 < NB:
                    search(b + 1)
                norm(b)
                if b + 1 < NB:
                    gates(b + 1)
                if b + 2 < NB:
                    project(b + 2)
                exponentials(b)
                if b + 2 < NB:
                    scores(b + 2)
                routed(b)
                if b + 2 < NB:
                    deviations(b + 2)

            act.wait_ge(S["slots_done"], 1)
            act.wait_ge(S["acc_out"], 16 * NB)
            act.wait_ge(S["xn2_out"], 16 * NB)
            act.wait_ge(S["bo_done"], NT)

            def load_slots(tile, k, buf, done):
                act.dma_start(buf[:, k, :], slot_d[bass.ds(tile * P, P), :]).then_inc(done[k], 16)

            def high_x(T, k):
                act.wait_ge(S["xT_ps"], T + 1)
                if not known(T, 2):
                    act.wait_ge(S["gu_ps"], T - 1)
                nc.scalar.copy(xh[:, k % 2, :], ps_x[:]).then_inc(S["xh_done"], 1)

            def high_h(T, k):
                act.wait_ge(S["hT_ps"], T + 1)
                if not known(T, 2):
                    act.wait_ge(S["y_ps"], T)
                nc.scalar.copy(hh[:, k % 2, :], ps_h[:]).then_inc(S["hh_done"], 1)

            def sigmoid(T, k):
                act.wait_ge(S["gc_done"], T + 1)
                if not known(T):
                    act.wait_ge(S["h_done"], T)
                nc.scalar.activation(sg[:], gc[:], ACT.Sigmoid, scale=ALPHA).then_inc(S["sg_done"], 1)

            def scale_y(T, k):
                act.wait_ge(aslot_in[k], slot_count(T, k))
                act.wait_ge(S["y_ps"], T + 2)
                if not known(T, 2):
                    act.wait_ge(S["added"], 16 * (T - 1))
                nc.scalar.mul(yb[:, k % 2, :], ps_y[k % 2][:],
                              aslot[:, k, 1:2].bitcast(fp32)).then_inc(S["y_done"], 1)

            def split_high(own, when):
                for h in range(2):
                    with act.If(field(act, own, f"{when}_{h}")):
                        buf = 1 - field(act, own, "buffer")
                        act.wait_ge(S[f"raw_in{h}"], (48, 32)[h] * field(act, own, "expert") + 2 * (48, 32)[h])
                        act.wait_ge(S["y_ps"], field(act, own, "start") + 1)
                        for c in range(HALF * h, HALF * (h + 1)):
                            nc.scalar.copy(w[:, bass.ds(buf, 1), 0, c, :].rearrange("p a d -> p (a d)"),
                                           raw_w[:, c, :]).then_inc(S["hi_done"], 1)

            def step(T, k):
                own, offs = word(act, 0, T), word(act, 1, T)
                load_slots(field(act, offs, "slots_3"), (k + 3) % UNROLL, gslot, gslot_in)
                if not known(T):
                    high_h(T - 1, (k - 1) % UNROLL)
                high_x(T + 1, (k + 1) % UNROLL)
                split_high(own, "early")
                sigmoid(T, k)
                if not known(T):
                    scale_y(T - 1, (k - 1) % UNROLL)
                split_high(own, "late")
                if not known(T, 3):
                    act.wait_ge(S["added"], 16 * (T - 2))
                load_slots(field(act, offs, "slots_1"), (k + 1) % UNROLL, aslot, aslot_in)

            load_slots(0, 0, gslot, gslot_in)
            load_slots(0, 0, aslot, aslot_in)
            act.wait_ge(S["table_done"], 1)
            final = final_lap(act)
            load_slots(field(act, word(act, 1, TABLE - 3 + 1), "slots_1"), 1, gslot, gslot_in)
            high_x(0, 0)
            load_slots(field(act, word(act, 1, TABLE - 3 + 2), "slots_1"), 2, gslot, gslot_in)
            for T in range(UNROLL):
                step(T, T)
            with act.Fori(1, final + 1) as lap:
                for k in range(UNROLL):
                    step(UNROLL * lap + k, k)
            high_h(UNROLL * final + (UNROLL - 1), UNROLL - 1)
            scale_y(UNROLL * final + (UNROLL - 1), UNROLL - 1)

        @block.tensor
        def _(pe):
            T_ = nc.tensor.transpose
            pe.wait_ge(S["pool_c"], 5)
            pe.wait_ge(S["const_in"], 96)
            T_(ps_k[:, 0:P], wq_sb[:], ident[:])
            T_(ps_k[:, P:2 * P], wk_sb[:], ident[:])
            for c in range(HC):
                last = T_(ps_rw[:, c * E:(c + 1) * E], rw_sb[:, c * P:(c + 1) * P], ident[0:E, 0:E])
            last.then_inc(S["wT_ps"], 1)
            pe.wait_ge(S["ctx_in_s"], 16)

            def project(b):
                if b:
                    pe.wait_ge(S["qk_done"], 2 * b)
                if b == 1:
                    pe.wait_ge(S["ctx_rest_in"], 16)
                for r in range(RT):
                    last = T_(ps_q[:, r * P:(r + 1) * P], ctx_sb[:, b * RT + r, :], ident[:])
                last.then_inc(S["ctxT_ps"], 1)
                pe.wait_ge(S["ctxT_done"], b + 1)
                if b == 0:
                    pe.wait_ge(S["wT_done"], 3)
                nc.tensor.matmul(ps_q[:], wqT[:], ctxT[:], start=True, stop=True).then_inc(S["q_ps"], 1)
                nc.tensor.matmul(ps_k[:], wkT[:], ctxT[:], start=True, stop=True).then_inc(S["k_ps"], 1)

            def scores(b):
                pe.wait_ge(S["qk_done"], 2 * b + 2)
                for r in range(RT):
                    i = RT * b + r
                    if i >= 2:
                        pe.wait_ge(S["s_done"], i - 1)
                    nc.tensor.matmul(ps_s[i % 2][:], qT[:, r * P:(r + 1) * P], kT[:], start=True, stop=True).then_inc(S["s_ps"], 1)

            def router_products(b, r):
                pe.wait_ge(S["xt_done"], RT * b + r + 1)
                for c in range(HC):
                    last = nc.tensor.matmul(ps_logit[:, r * E:(r + 1) * E], xn2T[:, r, c * P:(c + 1) * P],
                                            rwT[:, c * E:(c + 1) * E], start=(c == 0), stop=(c == HC - 1))
                return last

            def count_ok(b):
                pe.wait_ge(S["ok_done"], b + 1)
                if b >= 2:
                    pe.wait_ge(S["bo_done"], RT * (b - 1))
                nc.tensor.matmul(ps_ok, ones[:], okv[:], start=True, stop=True).then_inc(S["ok_ps"], 1)

            for b in range(2):
                project(b)
                scores(b)
            count_ok(0)
            for b in range(NB):
                pe.wait_ge(S["a_done"], RT * (b + 1))
                if b:
                    pe.wait_ge(S["scT_done"], b)
                if b:
                    pe.wait_ge(S["bo_done"], RT * b)
                for r in range(RT):
                    i = RT * b + r
                    if i >= 2:
                        pe.wait_ge(S["x1_done"], i - 1)
                    for j in range(RT):
                        last = T_(ps_t[r % 2][:, j * P:(j + 1) * P], A[:, j, r * P:(r + 1) * P], ident[:])
                    last.then_inc(S["at_ps"], 1)
                pe.wait_ge(S["x1_done"], RT * (b + 1))
                if b:
                    pe.wait_ge(S["payload_done"], b)
                for r in range(RT):
                    i = RT * b + r
                    pe.wait_ge(S["xn2_done"], i + 1)
                    if i >= 2:
                        pe.wait_ge(S["xt_done"], i - 1)
                    for c in range(HC):
                        last = T_(ps_t[r % 2][:, c * P:(c + 1) * P], xn2[:, r, c * P:(c + 1) * P], ident[:])
                    last.then_inc(S["xt_ps"], 1)
                for r in range(RT):
                    last = router_products(b, r)
                last.then_inc(S["logit_ps"], 1)
                if b + 1 < NB:
                    count_ok(b + 1)
                if b + 2 < NB:
                    project(b + 2)
                pe.wait_ge(S["hot_done"], b + 1)
                nc.tensor.matmul(ps_rank, lower[:], onehot[:].rearrange("p r e -> p (r e)"), start=True, stop=False)
                nc.tensor.matmul(ps_rank, ones[:], before[:, b * RT:(b + 1) * RT, :].rearrange("p r e -> p (r e)"),
                                 start=False, stop=True).then_inc(S["rank_ps"], 1)
                if b + 2 < NB:
                    scores(b + 2)
                pe.wait_ge(S["dense_done"], b + 1)
                pe.wait_ge(S["payload_done"], b + 1)
                for r in range(RT):
                    last = T_(ps_scT[:, r * P:(r + 1) * P], dense[:, r, :], ident[:])
                last.then_inc(S["scT_ps"], 1)
                pe.wait_ge(S["scT_done"], b + 1)
                if b == NB - 1:
                    nc.tensor.matmul(ps_rank[:, 0:E], ones[:], before[:, NT, :], start=True, stop=True).then_inc(S["cnt_ps"], 1)
                for r in range(RT):
                    i = RT * b + r
                    if i >= 2:
                        pe.wait_ge(S["bo_done"], i - 1)
                    nc.tensor.matmul(ps_bd[r % 2], denseT[:, r * P:(r + 1) * P], bd_sb[:], start=True, stop=True).then_inc(S["bd_ps"], 1)
            pe.sem_inc(S["y_ps"], 1)
            pe.wait_ge(S["bo_done"], NT)

            def tr_x(T, k):
                pe.wait_ge(gathered[k], slot_count(T, k))
                if not known(T):
                    pe.wait_ge(S["xl_done"], T)
                for c in range(HC):
                    last = T_(ps_x[:, c * P:(c + 1) * P], xg[:, k, c * P:(c + 1) * P], ident[:])
                last.then_inc(S["xT_ps"], 1)

            def tr_h(T, k):
                pe.wait_ge(S["h_done"], T + 1)
                if not known(T):
                    pe.wait_ge(S["hl_done"], T)
                for c in range(HC):
                    last = T_(ps_h[:, c * P:(c + 1) * P], hb[:, k % 2, c * P:(c + 1) * P], ident[:])
                last.then_inc(S["hT_ps"], 1)

            def product(out_ps, high, low, buf, cols):
                n_mm = 3 * HC
                m = 0
                for c in range(HC):
                    rows = slice(c * P, (c + 1) * P)
                    for lhs, part in ((high, 0), (high, 1), (low, 0)):
                        last = nc.tensor.matmul(out_ps, lhs[:, rows],
                                                w[:, bass.ds(buf, 1), part, c, cols].rearrange("p a d -> p (a d)"),
                                                start=(m == 0), stop=(m == n_mm - 1))
                        m += 1
                return last

            def gate_up(T, k, half, buf):
                cols = slice(half * 512, (half + 1) * 512)
                last = product(psG[k % 2][:, cols], xh[:, k % 2, :], xl[:, k % 2, :], buf, cols)
                if half:
                    last.then_inc(S["gu_ps"], 1)

            def down(T, k, buf):
                pe.wait_ge(S["hl_done"], T + 1)
                if not known(T, 2):
                    pe.wait_ge(S["y_done"], T - 1)
                product(ps_y[k % 2][:], hh[:, k % 2, :], hl[:, k % 2, :], buf, slice(GU, WIDE)).then_inc(S["y_ps"], 1)

            def step(T, k):
                own = word(pe, 0, T)
                buf, need = field(pe, own, "buffer"), HC * field(pe, own, "expert") + HC
                pe.wait_ge(S["lo_done"], need)
                pe.wait_ge(S["xl_done"], T + 1)
                if not known(T, 2):
                    pe.wait_ge(S["gu_read"], T - 1)
                gate_up(T, k, 0, buf)
                if not known(T):
                    tr_h(T - 1, (k - 1) % UNROLL)
                tr_x(T + 1, (k + 1) % UNROLL)
                gate_up(T, k, 1, buf)
                if not known(T):
                    down(T - 1, (k - 1) % UNROLL, field(pe, own, "buffer_before"))

            tr_x(0, 0)
            pe.wait_ge(S["table_done"], 1)
            final = final_lap(pe)
            for T in range(UNROLL):
                step(T, T)
            with pe.Fori(1, final + 1) as lap:
                for k in range(UNROLL):
                    step(UNROLL * lap + k, k)
            last_tile = UNROLL * final + (UNROLL - 1)
            buf = field(pe, word(pe, 0, last_tile), "buffer")
            tr_h(last_tile, UNROLL - 1)
            down(last_tile, UNROLL - 1, buf)

        @block.vector
        def _(dve):
            n = [0]
            V = nc.vector

            def link(ins):
                n[0] += 1
                ins.then_inc(S["chain"], 1)
                dve.wait_ge(S["chain"], n[0])

            def send(ins):
                n[0] += 1
                ins.then_inc(S["chain"], 1)

            def join():
                dve.wait_ge(S["chain"], n[0])

            dve.wait_ge(S["pool_c"], 13)
            link(V.memset(pad_rows, 0))
            link(V.memset(minus_big[:], -BIG))
            V.memset(zero_rows, 0.0).then_inc(S["dve_c"], 1)
            V.memset(eps_c[:], EPS).then_inc(S["dve_c"], 1)
            V.tensor_scalar(pad_rows[:, :, 0], pad_i, P - 1, TOKENS, ALU.bitwise_and, ALU.bitwise_or).then_inc(S["dve_c"], 1)
            V.memset(before[:, 0, :], 0.0).then_inc(S["dve_c"], 1)
            V.tensor_copy(payload[:, :, 0].rearrange("p (i k) -> p i k", k=TOP_K),
                          token_id[:].bitcast(u32).unsqueeze(2).broadcast_to([P, NT, TOP_K])).then_inc(S["dve_c"], 1)
            dve.wait_ge(S["wT_ps"], 1)
            V.tensor_copy(wqT[:], ps_k[:, 0:P]).then_inc(S["wT_done"], 1)
            V.tensor_copy(wkT[:], ps_k[:, P:2 * P]).then_inc(S["wT_done"], 1)
            V.tensor_copy(rwT[:], ps_rw).then_inc(S["wT_done"], 1)
            dve.wait_ge(S["gam_done"], 1)
            link(V.tensor_scalar(gam[:, 2:3], gam[:, 1:2], 0.5, None, ALU.mult))
            link(V.tensor_scalar(gam[:, 3:4], gam[:, 1:2], -1.0, 1.0, ALU.mult, ALU.add))

            def statistics(b):
                dve.wait_ge(x_in[b], 16)
                for r in range(RT):
                    send(V.bn_stats(st1[:, 1, r, :], x_sb[:, b * RT + r, :]))
                for r in range(RT):
                    dve.wait_ge(S["s_done"], RT * b + r + 1)
                    send(V.bn_stats(st1[:, 0, r, :], sim[:, b % 2, r, :]))
                join()
                for w in range(2):
                    for r in range(RT):
                        ins = V.bn_aggr(mv1[:, w, r, :], st1[:, w, r, :])
                        if w == 0 or r < RT - 1:
                            send(ins)
                join()
                ins.then_inc(S["var1"], 1)

            def first_guess(b):
                dve.wait_ge(S["sd1"], b + 1)
                send(V.tensor_scalar(slope[:, b % 2, :], sd1[:, 0, :], 1.0 / (N * DENSITY), None, ALU.mult))
                V.scalar_tensor_tensor(out=nguess[:, b % 2, :], in0=sd1[:, 0, :], scalar=-QUANTILE, in1=mv1[:, 0, :, 0],
                                       op0=ALU.mult, op1=ALU.subtract).then_inc(S["guess_done"], 1)
                link(V.reciprocal(rs[:], sd1[:, 1, :]))
                link(V.tensor_scalar(rs[:], rs[:], gam[:, 3:4], None, ALU.mult))
                link(V.scalar_tensor_tensor(out=b1[:, b % 2, :], in0=mv1[:, 1, :, 0], scalar=-1.0, in1=rs[:],
                                            op0=ALU.mult, op1=ALU.mult))
                V.tensor_scalar(s1[:, b % 2, :], rs[:], 1.0, None, ALU.add).then_inc(S["aff1"], 1)

            def thresholds(b):
                dve.wait_ge(S["moved"], 2 * len(GAINS) * (b + 1))
                link(V.tensor_scalar(guess[:], nguess[:, b % 2, :], -1.0, None, ALU.mult))
                for pair in range(0, RT, 2):
                    for r in (pair, pair + 1):
                        send(V.scalar_tensor_tensor(out=work[:, r % 2, :], in0=sim[:, b % 2, r, :], scalar=guess[:, r:r + 1],
                                                    in1=minus_big[:].broadcast_to([P, N]), op0=ALU.is_ge, op1=ALU.mult,
                                                    accum_out=above[:, r:r + 1]))
                    join()
                    for r in (pair, pair + 1):
                        send(V.tensor_tensor(work[:, r % 2, :], work[:, r % 2, :], sim[:, b % 2, r, :], ALU.add))
                    join()
                    for r in (pair, pair + 1):
                        send(V.max(top8[:, r, :], work[:, r % 2, :]))
                    join()
                link(V.tensor_scalar(above[:], above[:], 1.0 / BIG, float(KEEP - 1), ALU.mult, ALU.add))
                link(V.tensor_tensor(pick[:], iota8[:].unsqueeze(1).broadcast_to([P, RT, 8]),
                                     above[:].unsqueeze(2).broadcast_to([P, RT, 8]), ALU.is_equal))
                V.tensor_reduce(okv[:], pick[:], AX.X, ALU.add).then_inc(S["ok_done"], 1)
                dve.wait_ge(S["ok_done"], b + 1)
                link(V.tensor_tensor(pick[:], pick[:], top8[:], ALU.mult))
                link(V.tensor_reduce(thr[:], pick[:], AX.X, ALU.add))
                dve.wait_ge(S["ok_ps"], b + 1)
                link(V.tensor_reduce(okf[:], ps_ok, AX.X, ALU.add))
                link(V.tensor_scalar(oki[:], okf[:], float(P * RT), None, ALU.is_lt))
                failed = dve.value_load(oki[0:1, 0:1], min_val=0, max_val=1)
                with dve.If(failed):
                    for r in range(RT):
                        V.tensor_copy(work[:, 0, :], sim[:, b % 2, r, :])
                        dve.drain()
                        with dve.Fori(0, (KEEP - 1) // 8):
                            V.max(top8[:, r, :], work[:, 0, :])
                            dve.drain()
                            V.match_replace(work[:, 0, :], top8[:, r, :], work[:, 0, :], NEG)
                            dve.drain()
                        V.max(top8[:, r, :], work[:, 0, :])
                        dve.drain()
                        V.tensor_copy(thr[:, r:r + 1], top8[:, r, (KEEP - 1) % 8:(KEEP - 1) % 8 + 1])
                        dve.drain()

            def add_bias(b, r):
                dve.wait_ge(S["bd_ps"], RT * b + r + 1)
                V.tensor_tensor(base_out[:, r, :], ps_bd[r % 2], x1[:, r, :], ALU.add).then_inc(S["bo_done"], 1)

            statistics(0)
            first_guess(0)
            dve.wait_ge(S["ctxT_ps"], 2)
            V.tensor_copy(ctxT[:], ps_q[:]).then_inc(S["ctxT_done"], 1)
            dve.wait_ge(S["q_ps"], 2)
            V.tensor_copy(qT[:], ps_q[:]).then_inc(S["qk_done"], 1)
            dve.wait_ge(S["k_ps"], 2)
            V.tensor_copy(kT[:], ps_k[:]).then_inc(S["qk_done"], 1)
            for r in range(RT):
                dve.wait_ge(S["s_ps"], RT + r + 1)
                V.tensor_copy(sim[:, 1, r, :], ps_s[r % 2][:]).then_inc(S["s_done"], 1)
            statistics(1)
            first_guess(1)
            thresholds(0)
            for b in range(NB):
                dve.wait_ge(S["sig_done"], RT * (b + 1))
                for r in range(RT):
                    V.scalar_tensor_tensor(out=A[:, r, :], in0=sim[:, b % 2, r, :], scalar=thr[:, r:r + 1],
                                           in1=A[:, r, :], op0=ALU.is_ge, op1=ALU.mult).then_inc(S["a_done"], 1)
                dve.wait_ge(S["a_done"], RT * (b + 1))
                dve.wait_ge(S["base_done"], RT * (b + 1))
                for r in range(RT):
                    send(V.scalar_tensor_tensor(out=x_sb[:, RT * b + r, :], in0=A[:, r, :], scalar=gam[:, 2:3],
                                                in1=x_sb[:, RT * b + r, :], op0=ALU.mult, op1=ALU.add))
                join()
                if b:
                    dve.wait_ge(S["xn2_done"], RT * b)
                    dve.wait_ge(S["acc_out"], 16 * b)
                for r in range(RT):
                    dve.wait_ge(S["at_ps"], RT * b + r + 1)
                    V.scalar_tensor_tensor(out=x1[:, r, :], in0=ps_t[r % 2], scalar=gam[:, 2:3],
                                           in1=x_sb[:, RT * b + r, :], op0=ALU.mult, op1=ALU.add).then_inc(S["x1_done"], 1)
                dve.wait_ge(S["x1_done"], RT * (b + 1))
                for r in range(RT):
                    send(V.bn_stats(st[:, r, :], x1[:, r, :]))
                join()
                for r in range(RT):
                    ins = V.bn_aggr(mv[:, r, :], st[:, r, :])
                    if r < RT - 1:
                        send(ins)
                join()
                ins.then_inc(S["var2"], 1)
                dve.wait_ge(S["sd2"], b + 1)
                link(V.reciprocal(r2[:], sd[:]))
                link(V.tensor_tensor(b2[:], mv[:, :, 0], r2[:], ALU.mult))
                V.tensor_scalar(b2[:], b2[:], -1.0, None, ALU.mult).then_inc(S["aff2"], 1)
                if b + 1 < NB:
                    thresholds(b + 1)
                dve.wait_ge(S["logit_ps"], b + 1)
                link(V.tensor_tensor(logit[:], ps_logit.rearrange("p (r e) -> p r e", e=E),
                                     rb_sb[:].unsqueeze(1).broadcast_to([P, RT, E]), ALU.add))
                for r in range(RT):
                    send(V.max(best[:, r, :], logit[:, r, :]))
                join()
                for r in range(RT):
                    send(V.max_index(best_i[:, r, :], best[:, r, :], logit[:, r, :]))
                V.tensor_tensor(dl[:], best[:, :, 0:TOP_K], best[:, :, 0:1].broadcast_to([P, RT, TOP_K]),
                                ALU.subtract).then_inc(S["dl_done"], 1)
                join()
                link(V.tensor_copy(ek[:], best_i[:, :, 0:TOP_K]))
                link(V.tensor_tensor(hot[:].rearrange("p r k e -> p (r k) e"),
                                     iota_e[:].unsqueeze(1).broadcast_to([P, RT * TOP_K, E]),
                                     ek[:].rearrange("p r k -> p (r k)").unsqueeze(2).broadcast_to([P, RT * TOP_K, E]),
                                     ALU.is_equal))
                link(V.tensor_reduce(onehot[:], hot[:].rearrange("p r k e -> p r e k"), AX.X, ALU.add))
                for r in range(RT):
                    i = RT * b + r
                    ins = V.tensor_tensor(before[:, i + 1, :], before[:, i, :], onehot[:, r, :], ALU.add)
                    if r < RT - 1:
                        link(ins)
                ins.then_inc(S["hot_done"], 1)
                dve.wait_ge(S["ex_done"], b + 1)
                link(V.tensor_reduce(den[:], ex[:], AX.X, ALU.add))
                link(V.reciprocal(den[:], den[:]))
                link(V.tensor_tensor(score[:], ex[:], den[:].unsqueeze(2).broadcast_to([P, RT, TOP_K]), ALU.mult))
                link(V.tensor_tensor(hotv[:].rearrange("p r k e -> p (r k) e"), hot[:].rearrange("p r k e -> p (r k) e"),
                                     score[:].rearrange("p r k -> p (r k)").unsqueeze(2).broadcast_to([P, RT * TOP_K, E]),
                                     ALU.mult))
                V.tensor_reduce(dense[:], hotv[:].rearrange("p r k e -> p r e k"), AX.X, ALU.add).then_inc(S["dense_done"], 1)
                dve.wait_ge(S["dense_done"], b + 1)
                dve.wait_ge(S["rank_ps"], b + 1)
                link(V.tensor_tensor(pos[:], ps_rank.rearrange("p (r e) -> p r e", e=E),
                                     slot0_e[:].unsqueeze(1).broadcast_to([P, RT, E]), ALU.add))
                for r in range(RT):
                    send(V.tensor_tensor(hotv[:, r], hot[:, r], pos[:, r, :].unsqueeze(1).broadcast_to([P, TOP_K, E]), ALU.mult))
                join()
                link(V.tensor_reduce(posk[:], hotv[:], AX.X, ALU.add))
                sl = slice(b * RT * TOP_K, (b + 1) * RT * TOP_K)
                link(V.tensor_copy(slot_i[:, sl], posk[:].rearrange("p r k -> p (r k)")))
                V.tensor_copy(payload[:, sl, 1].bitcast(fp32), score[:].rearrange("p r k -> p (r k)")).then_inc(S["payload_done"], 1)
                dve.wait_ge(S["xn2_done"], RT * (b + 1))
                if b + 2 < NB:
                    statistics(b + 2)
                if b < NB - 1:
                    for r in range(RT):
                        add_bias(b, r)
                if b + 2 < NB:
                    first_guess(b + 2)

            dve.wait_ge(S["cnt_ps"], 1)
            link(V.tensor_copy(cnt[:], ps_rank[0:1, 0:E]))
            link(V.tensor_tensor(ncmp, cnt[:].unsqueeze(2).broadcast_to([1, E, E]),
                                 jtab[:].unsqueeze(1).broadcast_to([1, E, E]), ALU.is_gt))
            link(V.tensor_reduce(til[:], ncmp, AX.X, ALU.add))
            link(V.tensor_scalar(til[:], til[:], 1.0, None, ALU.max))
            link(V.tensor_copy(cum[:, 0, :], til[:]))
            src = 0
            for s in (1, 2, 4, 8):
                send(V.tensor_tensor(cum[:, 1 - src, s:E], cum[:, src, s:E], cum[:, src, 0:E - s], ALU.add))
                link(V.tensor_copy(cum[:, 1 - src, 0:s], cum[:, src, 0:s]))
                src = 1 - src
            add_bias(NB - 1, 0)
            add_bias(NB - 1, 1)
            link(V.tensor_scalar(lapj[:], lapj[:], cum[:, src, E - 1:E], None, ALU.is_lt))
            link(V.tensor_reduce(tf[:, 0, 0:1], lapj[:], AX.X, ALU.add))
            link(V.tensor_scalar(laps_tab[:], tf[:, 0, 0:1], -1.0, None, ALU.add))
            link(V.tensor_tensor(cmp_t, ttab[:].unsqueeze(2).broadcast_to([1, TABLE, E]),
                                 cum[:, src, :].unsqueeze(1).broadcast_to([1, TABLE, E]), ALU.is_ge))
            link(V.tensor_reduce(tf[:, 0, :], cmp_t, AX.X, ALU.add))
            add_bias(NB - 1, 2)
            add_bias(NB - 1, 3)
            link(V.tensor_tensor(cmp_w, cmp_t, til[:].unsqueeze(1).broadcast_to([1, TABLE, E]), ALU.mult))
            link(V.tensor_reduce(tf[:, 1, :], cmp_w, AX.X, ALU.add))
            link(V.tensor_scalar(tf[:, 2, :], tf[:, 0, :], 3.0, None, ALU.is_ge))
            for e in range(6, E, 3):
                link(V.scalar_tensor_tensor(out=tf[:, 2, :], in0=tf[:, 0, :], scalar=float(e), in1=tf[:, 2, :],
                                            op0=ALU.is_ge, op1=ALU.add))
            link(V.scalar_tensor_tensor(out=tf[:, 2, :], in0=tf[:, 2, :], scalar=-3.0, in1=tf[:, 0, :],
                                        op0=ALU.mult, op1=ALU.add))
            link(V.tensor_tensor(tf[:, 3, :], ttab[:], tf[:, 1, :], ALU.subtract))
            link(V.tensor_scalar(tf[:, 3, :], tf[:, 3, :], float(P), None, ALU.mult))
            link(V.scalar_tensor_tensor(out=tf[:, 3, :], in0=tf[:, 0, :], scalar=float(TOKENS), in1=tf[:, 3, :],
                                        op0=ALU.mult, op1=ALU.add))
            link(V.tensor_scalar(tf[:, 3, :], tf[:, 3, :], float(SLOTS), None, ALU.min))
            tabs = lambda row: tf[:, row, 0:TABLE - 1]
            fields = word_f[:, 0, 0:TABLE - 1]

            def put(name, value, into):
                return V.scalar_tensor_tensor(out=into, in0=value, scalar=float(1 << FIELDS[name][0]), in1=into,
                                              op0=ALU.mult, op1=ALU.add)

            link(V.tensor_tensor(tabs(4), tf[:, 0, 1:TABLE], tabs(0), ALU.subtract))
            link(V.tensor_tensor(tabs(5), ttab[:, 0:TABLE - 1], tabs(1), ALU.subtract))
            steps = slice(0, TABLE - 3)
            last, last_1, last_2 = (tf[:, 4, i:TABLE - 3 + i] for i in range(3))
            nth, splits, early, spare = tf[:, 5, steps], tf[:, 6, steps], tf[:, 7, steps], word_f[:, 0, steps]
            link(V.memset(tabs(6), 0.0))
            link(V.tensor_tensor(splits, last, last_1, ALU.max))
            link(V.scalar_tensor_tensor(out=splits, in0=splits, scalar=3.0, in1=last_2, op0=ALU.mult, op1=ALU.max))
            link(V.scalar_tensor_tensor(out=splits, in0=nth, scalar=0.0, in1=splits, op0=ALU.is_equal, op1=ALU.mult))
            link(V.tensor_scalar(early, last, -1.0, 1.0, ALU.mult, ALU.add))
            link(V.scalar_tensor_tensor(out=spare, in0=last_1, scalar=1.0, in1=early, op0=ALU.add, op1=ALU.mult))
            link(V.scalar_tensor_tensor(out=spare, in0=nth, scalar=1.0, in1=spare, op0=ALU.is_equal, op1=ALU.mult))
            link(V.scalar_tensor_tensor(out=early, in0=nth, scalar=2.0, in1=early, op0=ALU.is_equal, op1=ALU.mult))
            link(V.scalar_tensor_tensor(out=early, in0=early, scalar=2.0, in1=spare, op0=ALU.mult, op1=ALU.add))
            link(V.scalar_tensor_tensor(out=splits, in0=splits, scalar=4.0, in1=early, op0=ALU.mult, op1=ALU.add))
            link(V.scalar_tensor_tensor(out=tabs(6), in0=tabs(0), scalar=float(E - 1), in1=tabs(6),
                                        op0=ALU.is_lt, op1=ALU.mult))
            link(V.tensor_scalar(tf[:, 0, :], tf[:, 0, :], float(E - 1), None, ALU.min))
            link(V.tensor_copy(word_f[:, 0, :], tf[:, 0, :]))
            link(put("early_0", tabs(6), fields))
            link(put("start", tabs(1), fields))
            link(put("bias", tabs(2), fields))
            link(put("buffer_before", tabs(0), word_f[:, 0, 1:TABLE]))
            link(V.tensor_scalar(tabs(3), tabs(3), 1.0 / P, None, ALU.mult))
            link(V.scalar_tensor_tensor(out=word_f[:, 1, 0:TABLE - 4], in0=tf[:, 3, 3:TABLE - 1],
                                        scalar=float(1 << FIELDS["slots_3"][0]), in1=tf[:, 3, 1:TABLE - 3],
                                        op0=ALU.mult, op1=ALU.add))
            link(V.tensor_copy(word_f[:, 1, TABLE - 3:TABLE], tf[:, 3, 0:3]))
            V.tensor_copy(tile_tab[:], word_f).then_inc(S["table_done"], 1)
            dve.wait_ge(S["table_done"], 1)
            dve.wait_ge(S["slots_done"], 1)
            dve.wait_ge(S["acc_out"], 16 * NB)
            dve.wait_ge(S["xn2_out"], 16 * NB)

            c0 = n[0]

            def low_x(T, k):
                dve.wait_ge(S["xh_done"], T + 1)
                V.tensor_tensor(xl[:, k % 2, :], ps_x[:], xh[:, k % 2, :].bitcast(fp32),
                                ALU.subtract).then_inc(S["xl_done"], 1)

            def low_h(T, k):
                dve.wait_ge(S["hh_done"], T + 1)
                V.tensor_tensor(hl[:, k % 2, :], ps_h[:], hh[:, k % 2, :].bitcast(fp32),
                                ALU.subtract).then_inc(S["hl_done"], 1)

            def gate(T, k, bias):
                dve.wait_ge(S["gu_ps"], T + 1)
                V.tensor_tensor(gu[:], psG[k % 2][:], bgu[:, bass.ds(bias, 1), :].rearrange("p a d -> p (a d)"),
                                ALU.add).then_inc(S["gu_read"], 1)
                dve.wait_ge(S["gu_read"], T + 1)
                gv = gu[:].rearrange("p (d t) -> p t d", t=2)
                V.tensor_scalar(gc[:], gv[:, 0, :], LIMIT, None, ALU.min).then_inc(S["gc_done"], 1)
                V.tensor_scalar(uc[:], gv[:, 1, :], LIMIT, -LIMIT, ALU.min, ALU.max).then_inc(S["chain"], 1)
                dve.wait_ge(S["chain"], 2 * T + (c0 + 1))
                dve.wait_ge(S["gc_done"], T + 1)
                V.scalar_tensor_tensor(out=h1[:], in0=uc[:], scalar=1.0, in1=gc[:], op0=ALU.add,
                                       op1=ALU.mult).then_inc(S["chain"], 1)
                dve.wait_ge(S["chain"], 2 * T + (c0 + 2))
                dve.wait_ge(S["sg_done"], T + 1)
                if not known(T, 2):
                    dve.wait_ge(S["hT_ps"], T - 1)
                V.tensor_tensor(hb[:, k % 2, :], h1[:], sg[:], ALU.mult).then_inc(S["h_done"], 1)

            def split_low(own):
                for h in range(2):
                    early, late = FIELDS[f"early_{h}"][0], FIELDS[f"late_{h}"][0]
                    with dve.If(dve.snap(((own >> early) & 1) + ((own >> late) & 1))):
                        buf = dve.snap(1 - field(dve, own, "buffer"), min_val=0, max_val=1)
                        need = HC * field(dve, own, "expert") + HC
                        for c in range(HALF * h, HALF * (h + 1)):
                            dve.wait_ge(S["hi_done"], need + (c + 1))
                            V.tensor_tensor(w[:, bass.ds(buf, 1), 1, c, :].rearrange("p a d -> p (a d)"), raw_w[:, c, :],
                                            w[:, bass.ds(buf, 1), 0, c, :].rearrange("p a d -> p (a d)").bitcast(fp32),
                                            ALU.subtract).then_inc(S["lo_done"], 1)

            def step(T, k):
                own = word(dve, 0, T)
                if not known(T):
                    low_h(T - 1, (k - 1) % UNROLL)
                low_x(T + 1, (k + 1) % UNROLL)
                gate(T, k, field(dve, own, "bias"))
                split_low(own)

            final = final_lap(dve)
            low_x(0, 0)
            for T in range(UNROLL):
                step(T, T)
            with dve.Fori(1, final + 1) as lap:
                for k in range(UNROLL):
                    step(UNROLL * lap + k, k)
            low_h(UNROLL * final + (UNROLL - 1), UNROLL - 1)


_INS = ["x", "ctx_512", "L0_xattn_Wq", "L0_xattn_Wk", "L0_xattn_gamma_raw", "L0_ffn_router_weight",
        "L0_ffn_router_bias", "L0_ffn_gate_up_proj", "L0_ffn_gate_up_proj_bias", "L0_ffn_down_proj",
        "L0_ffn_down_proj_bias"]
_OUTS = [((4, 512, 512), "float32")]


def kernel(**inputs):
    import numpy as _np
    import concourse.bacc as _bacc
    from concourse import mybir as _mybir
    from concourse.bass_utils import run_bass_kernel_spmd as _run

    nc = _bacc.Bacc("TRN2", target_bir_lowering=False, num_devices=1)
    arrays, args = {}, []
    for name in _INS:
        a = _np.ascontiguousarray(_np.atleast_1d(_np.asarray(inputs[name])))
        arrays[f"in_{name}_dram"] = a
        args.append(nc.dram_tensor(f"in_{name}_dram", a.shape, _mybir.dt.from_np(a.dtype), kind="ExternalInput").ap())
    for i, (shape, dtype) in enumerate(_OUTS):
        dt = _mybir.dt.from_np(_np.dtype(dtype))
        args.append(nc.dram_tensor(f"out_{i}_dram", shape, dt, kind="ExternalOutput").ap())
    xattn_moe_kernel(nc, *args)
    r = _run(nc, [arrays], core_ids=[0])
    return r.results[0]["out_0_dram"]
```
